# Optimizing a Trainium2 kernel written in Bass

```python
import numpy as np
import jax
import jax.numpy as jnp

def _softmax(x, axis=-1):
    return jax.nn.softmax(x, axis=axis)
def _gelu(x):
    return jax.nn.gelu(x, approximate=True)
def _silu(x):
    return jax.nn.silu(x)
def _sigmoid(x):
    return jax.nn.sigmoid(x)
def _layernorm(x, axis=-1, eps=1e-5):
    m = jnp.mean(x, axis=axis, keepdims=True)
    v = jnp.var(x, axis=axis, keepdims=True)
    return (x - m) / jnp.sqrt(v + eps)
def _scatter_add(tgt, idx, src, axis=0):
    return tgt.at[idx].add(src)
def _segment_sum(src, seg, n):
    return jax.ops.segment_sum(src, seg, n)

kernel_name = 'mk_conv_preact_d1_conv_nchw128_7919fc'

def setup_inputs(seed: int = 0):
    np.random.seed(seed)
    _w = jnp.asarray
    def _rec_inputs():
        import jax
        import jax.numpy as jnp
        _gk = jax.random.key(seed)
        x = -0.0002091 + 1 * jax.random.normal(jax.random.fold_in(_gk, 1), (16, 128, 112, 112), jnp.float32)
        return x
    x = _rec_inputs()
    def _L0_conv_setup():
        import jax, jax.numpy as jnp
        import numpy as np
        BLOCK = 4
        KEEP = 2

        def nm_sparsify_last(t, m=BLOCK, n=KEEP):
            shape = t.shape
            b = t.reshape(-1, m)
            a = jnp.abs(b)
            topv, _ = jax.lax.top_k(a, n)
            thr = topv[:, n - 1:n]
            keep = (a >= thr) & (a != 0.0)
            return jnp.where(keep, b, 0.0).reshape(shape)

        def sparsify_input(x):
            xc = jnp.transpose(x, (0, 2, 3, 1))
            xc = nm_sparsify_last(xc)
            return jnp.transpose(xc, (0, 3, 1, 2))

        def sparsify_weight(w):
            wc = jnp.transpose(w, (0, 2, 3, 1))
            wc = nm_sparsify_last(wc)
            return jnp.transpose(wc, (0, 3, 1, 2))
        key = jax.random.key(seed)
        k1, k2, k3 = jax.random.split(key, 3)
        x = jax.random.normal(k1, (16, 128, 112, 112), dtype=jnp.float32)
        weight = jax.random.normal(k2, (128, 128, 3, 3), dtype=jnp.float32) * 0.05
        bias_p = jax.random.normal(k3, (128,), dtype=jnp.float32)
        return {'x': x, 'weight': weight, 'bias_p': bias_p}
    _L0_conv_all = _L0_conv_setup()
    _L0_conv_in = {k: v for k, v in _L0_conv_all.items() if k in ('weight', 'bias_p', )}
    del _L0_conv_all

    return {
        "x": x,
        "L0_conv_weight": _L0_conv_in["weight"],
        "L0_conv_bias_p": _L0_conv_in["bias_p"],
    }

def reference(x, L0_conv_weight, L0_conv_bias_p):
    import jax
    import jax.numpy as jnp
    def _L0_conv_ref(x, weight, bias_p):
        import jax, jax.numpy as jnp
        import numpy as np
        BLOCK = 4
        KEEP = 2

        def nm_sparsify_last(t, m=BLOCK, n=KEEP):
            shape = t.shape
            b = t.reshape(-1, m)
            a = jnp.abs(b)
            topv, _ = jax.lax.top_k(a, n)
            thr = topv[:, n - 1:n]
            keep = (a >= thr) & (a != 0.0)
            return jnp.where(keep, b, 0.0).reshape(shape)

        def sparsify_input(x):
            xc = jnp.transpose(x, (0, 2, 3, 1))
            xc = nm_sparsify_last(xc)
            return jnp.transpose(xc, (0, 3, 1, 2))

        def sparsify_weight(w):
            wc = jnp.transpose(w, (0, 2, 3, 1))
            wc = nm_sparsify_last(wc)
            return jnp.transpose(wc, (0, 3, 1, 2))
        xs = sparsify_input(x)
        ws = sparsify_weight(weight)
        out = jax.lax.conv_general_dilated(xs, ws, window_strides=(1, 1), padding=((1, 1), (1, 1)), lhs_dilation=(1, 1), rhs_dilation=(1, 1), dimension_numbers=('NCHW', 'OIHW', 'NCHW'), feature_group_count=1)
        return out + bias_p[None, :, None, None]

    def _gn(v, G=32, eps=1e-5):
        B_, C_, H_, W_ = v.shape
        g = v.reshape(B_, G, C_ // G, H_, W_)
        m = jnp.mean(g, axis=(2, 3, 4), keepdims=True)
        s = jnp.var(g, axis=(2, 3, 4), keepdims=True)
        return ((g - m) / jnp.sqrt(s + eps)).reshape(v.shape)

    def _ln_c(v, eps=1e-6):
        m = jnp.mean(v, axis=1, keepdims=True)
        s = jnp.var(v, axis=1, keepdims=True)
        return (v - m) / jnp.sqrt(s + eps)

    def _ln_t(v, eps=1e-5):
        m = jnp.mean(v, axis=-1, keepdims=True)
        s = jnp.var(v, axis=-1, keepdims=True)
        return (v - m) / jnp.sqrt(s + eps)

    def _to_tokens(v):
        B_, C_, H_, W_ = v.shape
        return v.reshape(B_, C_, H_ * W_).transpose(0, 2, 1)
    def _from_tokens(t, like):
        B_, C_, H_, W_ = like.shape
        return t.transpose(0, 2, 1).reshape(B_, C_, H_, W_)

    x = x + _L0_conv_ref(_gn(x), L0_conv_weight, L0_conv_bias_p)
    return x


_drawn_inputs = setup_inputs


def setup_inputs(seed=0):
    import zlib

    import numpy as np

    out = dict(_drawn_inputs(seed))
    spreads = {}
    factors = {}
    for name, (base, spread) in spreads.items():
        noise = np.random.default_rng([zlib.crc32(name.encode()), seed]).standard_normal(out[name].shape)
        drawn = base * np.exp(spread * noise) if base else spread * noise
        out[name] = jnp.asarray(drawn.astype(out[name].dtype))
    for name, factor in factors.items():
        out[name] = (out[name] * factor).astype(out[name].dtype)
    return out
```

```python
from contextlib import ExitStack

import numpy as np

import concourse.bass as bass
from concourse import mybir

ALU = mybir.AluOpType
ACT = mybir.ActivationFunctionType
F32 = mybir.dt.float32
F16 = mybir.dt.float16
U32 = mybir.dt.uint32
U8 = mybir.dt.uint8

P = 128
IMAGES, H, W = 16, 112, 112
PIX = H * W
BLOCK = 4
GROUPS = P // BLOCK
TAPS = 9
EPS = 1e-5

CHUNKS = 4
CROWS = H // CHUNKS
CPIX = CROWS * W
QUARTERS = P // GROUPS
QPIX = CPIX // QUARTERS
TROWS = 4
TPIX = TROWS * W
TILES = CROWS // TROWS
MOVED = 16 * BLOCK * QUARTERS
BN = 448
BNS = CPIX // BN

XSCALE = 256.0
WSCALE = 4096.0
TINY = 2.0 ** -100


def conv_kernel(nc, x, weight, bias, ident, avg_chan, avg_block, out):
    x_chan = x.rearrange("b c h w -> b c (h w)")
    out_chan = out.rearrange("b c h w -> b c (h w)")
    x_block = x.rearrange("b (g j) h w -> b g j (h w)", j=BLOCK)
    w_rows = weight.rearrange("o c kh kw -> o (c kh kw)")
    bias_col = bias.rearrange("(p a) -> p a", a=1)

    with ExitStack() as ctx:
        def sb(name, shape, dt):
            return ctx.enter_context(nc.sbuf_tensor(name, shape, dt))

        def sem(name):
            return ctx.enter_context(nc.semaphore(name))

        xs = sb("xs", [P, 2, PIX], F32)
        x_hi = sb("x_hi", [P, H, W], F16)
        x_lo = sb("x_lo", [P, H, W], F16)
        xb = sb("xb", [P, BLOCK, QPIX], F32)
        tmp = sb("tmp", [P, BLOCK, QPIX], F32)
        mask_b = sb("mask_b", [P, BLOCK, QPIX], U8)
        mask_c = sb("mask_c", [P, CPIX], U8)
        z = sb("z", [P, CPIX], F32)
        stage = sb("stage", [P, CPIX], F32)
        w_hi = sb("w_hi", [P, TAPS, P], F16)
        w_lo = sb("w_lo", [P, TAPS, P], F16)
        ident_s = sb("ident_s", [P, P], F16)
        avg_c = sb("avg_c", [P, P], F32)
        avg_b = sb("avg_b", [P, P], F32)
        bias_s = sb("bias_s", [P, 1], F32)
        w_pow = sb("w_pow", [P, 4], F32)
        bstat = sb("bstat", [P, CHUNKS * BNS, 6], F32)
        cstat = sb("cstat", [P, 2], F32)
        small = sb("small", [P, 6], F32)
        params = sb("params", [P, 2, 3], F32)

        banks = ctx.enter_context(nc.psum_tensor("banks", [P, TILES, 512], F32))
        spare = ctx.enter_context(nc.psum_tensor("spare", [P, 512], F32))
        w_trans = banks[:, :, :].bitcast(F16)

        wraw = xs[:, 1, 0:P * TAPS]
        wabs = xs[:, 1, 1152:2304]
        wmin = xs[:, 1, 2304:2880]
        wmax = xs[:, 1, 2880:3456]
        wmask = xs[:, 1, 3456:4608]
        wsp = xs[:, 1, 4608:5760]
        whr = xs[:, 1, 5760:6336].bitcast(F16)
        wlr = xs[:, 1, 6336:6912].bitcast(F16)

        consts_in = sem("consts_in")
        x_loaded = [[sem(f"x_loaded{p}{k}") for k in range(CHUNKS)] for p in range(2)]
        stored = [[sem(f"stored{p}{k}") for k in range(CHUNKS)] for p in range(2)]
        xb_loaded = sem("xb_loaded")
        w_step = sem("w_step")
        w_abs_done = sem("w_abs_done")
        w_ready = sem("w_ready")
        w_turned = sem("w_turned")
        w_kept = sem("w_kept")
        bn_done = sem("bn_done")
        chan_stats = sem("chan_stats")
        group_mean = sem("group_mean")
        mean_kept = sem("mean_kept")
        negmean_kept = sem("negmean_kept")
        mean_off = sem("mean_off")
        chan_var = sem("chan_var")
        group_var = sem("group_var")
        var_eps = sem("var_eps")
        root = sem("root")
        inv_root = sem("inv_root")
        root_twice = sem("root_twice")
        inv_twice = sem("inv_twice")
        scale_kept = sem("scale_kept")
        abs_done = sem("abs_done")
        pair_min = sem("pair_min")
        pair_max = sem("pair_max")
        max_of_min = sem("max_of_min")
        min_of_max = sem("min_of_max")
        thr_done = sem("thr_done")
        mask_done = sem("mask_done")
        mask_moved = sem("mask_moved")
        z_done = sem("z_done")
        hi_done = sem("hi_done")
        lo_done = sem("lo_done")
        tile_done = sem("tile_done")
        bank_free = sem("bank_free")
        resid_done = sem("resid_done")

        block = ctx.enter_context(nc.Block())

        def image_loop(eng, image):
            with eng.Fori(0, IMAGES // 2 - 1) as i:
                image(i, 0, False, False)
                image(i, 1, False, False)
            image(IMAGES // 2 - 1, 0, True, False)
            image(IMAGES // 2 - 1, 1, True, True)

        def pix(k):
            return slice(k * CPIX, (k + 1) * CPIX)

        @block.sync
        def _(sp):
            def load_x(b, p, k):
                sp.dma_start(xs[:, p, pix(k)], x_chan[b, :, pix(k)]).then_inc(x_loaded[p][k], 16)

            def load_block(b, k):
                for q in range(QUARTERS):
                    px = slice(k * CPIX + q * QPIX, k * CPIX + (q + 1) * QPIX)
                    sp.dma_start(xb[GROUPS * q:GROUPS * (q + 1), :, :],
                                 x_block[b, :, :, px]).then_inc(xb_loaded, 16)

            def move_mask(c):
                sp.wait_ge(mask_done, c + 1)
                for q in range(QUARTERS):
                    for j in range(BLOCK):
                        sp.dma_start(mask_c[j::BLOCK, q * QPIX:(q + 1) * QPIX],
                                     mask_b[GROUPS * q:GROUPS * (q + 1), j, :]).then_inc(mask_moved, 16)

            sp.dma_start(wraw, w_rows).then_inc(consts_in, 16)
            sp.dma_start(bias_s[:, :], bias_col).then_inc(consts_in, 16)
            sp.dma_start(ident_s[:, :], ident).then_inc(consts_in, 16)
            sp.dma_start(avg_c[:, :], avg_chan).then_inc(consts_in, 16)
            sp.dma_start(avg_b[:, :], avg_block).then_inc(consts_in, 16)
            for k in range(CHUNKS):
                load_x(0, 0, k)
            load_block(0, 0)
            sp.wait_ge(w_turned, 2 * TAPS)
            for k in range(CHUNKS):
                load_x(1, 1, k)
            for c in range(2):
                move_mask(c)
                load_block(0, c + 1)

            def image(i, p, last_pair, last):
                b = 2 * i + p
                for s in range(CHUNKS):
                    t = CHUNKS * b + s
                    if not (last and s >= 2):
                        move_mask(t + 2)
                    if not (last and s >= 1):
                        load_block(*((b, s + 3) if s == 0 else (b + 1, s - 1)))
                    if not last_pair:
                        sp.wait_ge(stored[p][s], 16 * (i + 1))
                        load_x(b + 2, p, s)

            image_loop(sp, image)
            for p in range(2):
                for k in range(CHUNKS):
                    sp.wait_ge(stored[p][k], 16 * (IMAGES // 2))

        @block.scalar
        def _(act):
            def absolute(c, i, p, first):
                act.wait_ge(xb_loaded, 64 * (c + 1))
                if first:
                    act.wait_ge(negmean_kept, 2 * i + p + 1)
                nc.scalar.activation(xb[:, :, :], xb[:, :, :], ACT.Abs, bias=params[:, p, 1:2],
                                     scale=1.0).then_inc(abs_done, 1)

            def high(c, k, p):
                act.wait_ge(z_done, c + 1)
                rows = x_hi[:, k * CROWS:(k + 1) * CROWS, :].rearrange("p h w -> p (h w)")
                nc.scalar.activation(rows, z[:, :], ACT.Copy, scale=params[:, p, 2:3]).then_inc(hi_done, 1)

            def square_root(n):
                act.wait_ge(var_eps, n + 1)
                nc.scalar.activation(small[:, 3:4], small[:, 2:3], ACT.Sqrt).then_inc(root, 1)

            def evacuate(t, j):
                act.wait_ge(tile_done, TILES * t + j + 1)
                nc.scalar.activation(stage[:, j * TPIX:(j + 1) * TPIX], banks[:, j, 0:TPIX], ACT.Identity,
                                     bias=bias_s[:, 0:1], scale=w_pow[:, 3:4]).then_inc(bank_free, 1)

            act.sem_inc(bank_free, TILES)
            act.wait_ge(consts_in, 80)
            nc.scalar.activation(wabs, wraw, ACT.Abs).then_inc(w_abs_done, 1)
            square_root(0)
            for c in range(2):
                absolute(c, 0, 0, c == 0)
                if c == 0:
                    act.wait_ge(scale_kept, 1)
                high(c, c, 0)
            act.wait_ge(w_step, 13)

            def image(i, p, last_pair, last):
                b = 2 * i + p
                for s in range(CHUNKS):
                    t = CHUNKS * b + s
                    prep = not (last and s >= 2)
                    ni, np_ = (i, p) if s < 2 else (i + p, 1 - p)
                    if prep:
                        absolute(t + 2, ni, np_, s == 2)
                    evacuate(t, 0)
                    if s == 2 and not last:
                        square_root(b + 1)
                    evacuate(t, 1)
                    evacuate(t, 2)
                    if prep:
                        if s == 2:
                            act.wait_ge(scale_kept, b + 2)
                        high(t + 2, (s + 2) % CHUNKS, np_)
                    for j in range(3, TILES):
                        evacuate(t, j)
                    act.wait_ge(resid_done, t + 1)
                    act.dma_start(out_chan[b, :, pix(s)], xs[:, p, pix(s)]).then_inc(stored[p][s], 16)

            image_loop(act, image)

        @block.vector
        def _(dve):
            V = nc.vector

            def stats(i, p, k):
                dve.wait_ge(x_loaded[p][k], 16 * (i + 1))
                for m in range(BNS):
                    at = k * CPIX + m * BN
                    ins = V.bn_stats(out=bstat[:, k * BNS + m, :], in_=xs[:, p, at:at + BN])
                ins.then_inc(bn_done, 1)

            def channel_stats(n):
                V.bn_aggr(out=cstat[:, :], in_=bstat[:, :, :].rearrange("p a b -> p (a b)")).then_inc(chan_stats, 1)

            def keep_means(n, p):
                dve.wait_ge(group_mean, n + 1)
                V.tensor_copy(params[:, p, 0:1], spare[:, 0:1]).then_inc(mean_kept, 1)
                V.tensor_scalar(params[:, p, 1:2], spare[:, 1:2], -1.0, None, ALU.mult).then_inc(negmean_kept, 1)
                dve.wait_ge(mean_kept, n + 1)
                V.tensor_tensor(small[:, 0:1], cstat[:, 0:1], params[:, p, 0:1], ALU.subtract).then_inc(mean_off, 1)
                dve.wait_ge(mean_off, n + 1)
                V.scalar_tensor_tensor(out=small[:, 1:2], in0=small[:, 0:1], scalar=small[:, 0:1],
                                       in1=cstat[:, 1:2], op0=ALU.mult, op1=ALU.add).then_inc(chan_var, 1)

            def keep_scale(n, p):
                dve.wait_ge(group_var, n + 1)
                V.tensor_scalar(small[:, 2:3], spare[:, 2:3], EPS, None, ALU.add).then_inc(var_eps, 1)
                dve.wait_ge(root, n + 1)
                V.reciprocal(small[:, 4:5], small[:, 3:4]).then_inc(inv_root, 1)
                dve.wait_ge(inv_root, n + 1)
                V.scalar_tensor_tensor(out=small[:, 5:6], in0=small[:, 2:3], scalar=small[:, 4:5],
                                       in1=small[:, 3:4], op0=ALU.mult, op1=ALU.add).then_inc(root_twice, 1)
                dve.wait_ge(root_twice, n + 1)
                V.reciprocal(small[:, 4:5], small[:, 5:6]).then_inc(inv_twice, 1)
                dve.wait_ge(inv_twice, n + 1)
                V.tensor_scalar(params[:, p, 2:3], small[:, 4:5], 2.0 * XSCALE, None, ALU.mult).then_inc(scale_kept, 1)

            def find_mask(c):
                dve.wait_ge(abs_done, c + 1)
                V.tensor_tensor(tmp[:, 0:2, :], xb[:, 0:2, :], xb[:, 2:4, :], ALU.min).then_inc(pair_min, 1)
                V.tensor_tensor(tmp[:, 2:4, :], xb[:, 0:2, :], xb[:, 2:4, :], ALU.max).then_inc(pair_max, 1)
                dve.wait_ge(pair_min, c + 1)
                V.tensor_tensor(tmp[:, 0, :], tmp[:, 0, :], tmp[:, 1, :], ALU.max).then_inc(max_of_min, 1)
                dve.wait_ge(pair_max, c + 1)
                V.tensor_tensor(tmp[:, 2, :], tmp[:, 2, :], tmp[:, 3, :], ALU.min).then_inc(min_of_max, 1)
                dve.wait_ge(max_of_min, c + 1)
                dve.wait_ge(min_of_max, c + 1)
                V.tensor_tensor(tmp[:, 1, :], tmp[:, 0, :], tmp[:, 2, :], ALU.max).then_inc(thr_done, 1)
                dve.wait_ge(thr_done, c + 1)
                dve.wait_ge(mask_moved, MOVED * c)
                V.tensor_tensor(mask_b[:, :, :], xb[:, :, :], tmp[:, 1:2, :].to_broadcast([P, BLOCK, QPIX]),
                                ALU.is_ge).then_inc(mask_done, 1)

            def sparse(c, k, p):
                dve.wait_ge(mask_moved, MOVED * (c + 1))
                V.scalar_tensor_tensor(out=z[:, :], in0=xs[:, p, pix(k)], scalar=params[:, p, 0:1],
                                       in1=mask_c[:, :], op0=ALU.subtract, op1=ALU.mult).then_inc(z_done, 1)

            def low(c, k, p):
                dve.wait_ge(hi_done, c + 1)
                hi = x_hi[:, k * CROWS:(k + 1) * CROWS, :].rearrange("p h w -> p (h w)")
                lo = x_lo[:, k * CROWS:(k + 1) * CROWS, :].rearrange("p h w -> p (h w)")
                V.scalar_tensor_tensor(out=lo, in0=z[:, :], scalar=params[:, p, 2:3], in1=hi,
                                       op0=ALU.mult, op1=ALU.subtract).then_inc(lo_done, 1)

            def residual(t, k, p):
                dve.wait_ge(bank_free, TILES * (t + 2))
                V.tensor_tensor(xs[:, p, pix(k)], xs[:, p, pix(k)], stage[:, :], ALU.add).then_inc(resid_done, 1)

            steps = [0]

            def step(ins):
                steps[0] += 1
                ins.then_inc(w_step, 1)
                dve.wait_ge(w_step, steps[0])

            g4 = lambda v: v.rearrange("o (g j t) -> o g j t", j=BLOCK, t=TAPS)
            g2 = lambda v: v.rearrange("o (g j t) -> o g j t", j=2, t=TAPS)
            dve.wait_ge(w_abs_done, 1)
            step(V.tensor_tensor(g2(wmin), g4(wabs)[:, :, 0:2, :], g4(wabs)[:, :, 2:4, :], ALU.min))
            step(V.tensor_tensor(g2(wmax), g4(wabs)[:, :, 0:2, :], g4(wabs)[:, :, 2:4, :], ALU.max))
            step(V.tensor_tensor(g2(wmin)[:, :, 0, :], g2(wmin)[:, :, 0, :], g2(wmin)[:, :, 1, :], ALU.max))
            step(V.tensor_tensor(g2(wmax)[:, :, 0, :], g2(wmax)[:, :, 0, :], g2(wmax)[:, :, 1, :], ALU.min))
            step(V.tensor_tensor(g2(wmin)[:, :, 0, :], g2(wmin)[:, :, 0, :], g2(wmax)[:, :, 0, :], ALU.max))
            for j in range(BLOCK):
                ins = V.tensor_tensor(g4(wmask)[:, :, j, :], g4(wabs)[:, :, j, :], g2(wmin)[:, :, 0, :], ALU.is_ge)
                if j < BLOCK - 1:
                    ins.then_inc(w_step, 1)
                    steps[0] += 1
            step(ins)
            V.tensor_reduce(w_pow[:, 0:1], wabs, mybir.AxisListType.X, ALU.max).then_inc(w_step, 1)
            steps[0] += 1
            step(V.tensor_tensor(wsp, wraw, wmask, ALU.mult))
            step(V.tensor_scalar(w_pow[:, 0:1], w_pow[:, 0:1], TINY, None, ALU.max))
            step(V.tensor_scalar(w_pow[:, 1:2].bitcast(U32), w_pow[:, 0:1].bitcast(U32), 0x7F800000, None,
                                 ALU.bitwise_and))
            step(V.reciprocal(w_pow[:, 2:3], w_pow[:, 1:2]))
            step(V.tensor_scalar(w_pow[:, 3:4], w_pow[:, 1:2], 1.0 / (XSCALE * WSCALE), None, ALU.mult))
            step(V.tensor_scalar(wsp, wsp, w_pow[:, 2:3], WSCALE, ALU.mult, ALU.mult))
            step(V.tensor_copy(whr, wsp))
            V.tensor_tensor(wlr, wsp, whr, ALU.subtract).then_inc(w_ready, 1)
            for n in range(2 * TAPS):
                dve.wait_ge(w_turned, n + 1)
                dst = (w_hi if n < TAPS else w_lo)[:, n % TAPS, :]
                V.tensor_copy(dst, w_trans[:, n % TILES, 0:P]).then_inc(w_kept, 1)

            for k in range(CHUNKS):
                stats(0, 0, k)
            dve.wait_ge(bn_done, CHUNKS)
            channel_stats(0)
            keep_means(0, 0)
            keep_scale(0, 0)
            for c in range(2):
                find_mask(c)
                sparse(c, c, 0)
                low(c, c, 0)
            stats(0, 1, 0)

            def image(i, p, last_pair, last):
                b = 2 * i + p
                for s in range(CHUNKS):
                    t = CHUNKS * b + s
                    prep = not (last and s >= 2)
                    np_ = p if s < 2 else 1 - p
                    if prep:
                        find_mask(t + 2)
                    if s < 2 and not last:
                        stats(i + p, 1 - p, s + 1)
                    if s == 3 and not last_pair:
                        stats(i + 1, p, 0)
                    if s == 2 and not last:
                        keep_scale(b + 1, 1 - p)
                    if prep:
                        sparse(t + 2, (s + 2) % CHUNKS, np_)
                    if s == 1 and not last:
                        stats(i + p, 1 - p, 3)
                    if s == 1 and not last:
                        dve.wait_ge(bn_done, CHUNKS * (b + 2))
                    if prep:
                        low(t + 2, (s + 2) % CHUNKS, np_)
                    if s == 1 and not last:
                        channel_stats(b + 1)
                        keep_means(b + 1, 1 - p)
                    residual(t, s, p)

            image_loop(dve, image)

        @block.tensor
        def _(pe):
            def mean_products(n):
                pe.wait_ge(chan_stats, n + 1)
                nc.tensor.matmul(spare[:, 0:1], avg_c[:, :], cstat[:, 0:1], start=True, stop=True)
                nc.tensor.matmul(spare[:, 1:2], avg_b[:, :], cstat[:, 0:1], start=True, stop=True).then_inc(group_mean, 1)

            def var_product(n):
                pe.wait_ge(chan_var, n + 1)
                nc.tensor.matmul(spare[:, 2:3], avg_c[:, :], small[:, 1:2], start=True, stop=True).then_inc(group_var, 1)

            def tile(b, s, j):
                r0 = s * CROWS + j * TROWS
                pe.wait_ge(bank_free, 28 * b + TILES * s + j + 1)
                taps = [(0, 0)] + [(dy, dx) for dy in (-1, 0, 1) for dx in (-1, 0, 1) if (dy, dx) != (0, 0)]
                view = banks[:, j, 0:TPIX].rearrange("p (r w) -> p r w", w=W)
                for n, (dy, dx) in enumerate(taps):
                    a, e = max(0, -dy - r0), min(TROWS, H - dy - r0)
                    u, v = max(0, -dx), min(W, W - dx)
                    tap = (dy + 1) * 3 + dx + 1
                    dst = view[:, a:e, u:v]
                    rows, cols = slice(r0 + dy + a, r0 + dy + e), slice(u + dx, v + dx)
                    for m, (wt, xt) in enumerate(((w_hi, x_hi), (w_lo, x_hi), (w_hi, x_lo))):
                        last = n == TAPS - 1 and m == 2
                        ins = nc.tensor.matmul(dst, wt[:, tap, :], xt[:, rows, cols], start=(n == 0 and m == 0),
                                               stop=last)
                ins.then_inc(tile_done, 1)

            pe.wait_ge(w_ready, 1)
            for n in range(2 * TAPS):
                src = (whr if n < TAPS else wlr).rearrange("o (c t) -> o c t", t=TAPS)[:, :, n % TAPS]
                if n >= TILES:
                    pe.wait_ge(w_kept, n - TILES + 1)
                nc.tensor.transpose(w_trans[:, n % TILES, 0:P], src, ident_s[:, :]).then_inc(w_turned, 1)
            pe.wait_ge(w_kept, 2 * TAPS)
            mean_products(0)
            var_product(0)

            def image(b, last):
                for s in range(CHUNKS):
                    if s == 0:
                        pe.wait_ge(lo_done, CHUNKS * b + 1)
                    for j in range(TILES):
                        if s == 1 and j == TILES - 1 and not last:
                            mean_products(b + 1)
                        if s == 2 and j == 1 and not last:
                            var_product(b + 1)
                        if j == TILES - 1 and s < CHUNKS - 1:
                            pe.wait_ge(lo_done, CHUNKS * b + s + 2)
                        tile(b, s, j)

            with pe.Fori(0, IMAGES - 1) as b:
                image(b, False)
            image(IMAGES - 1, True)


_OUT = (IMAGES, P, H, W)


def kernel(x, L0_conv_weight, L0_conv_bias_p):
    import concourse.bacc as bacc
    from concourse.bass_utils import run_bass_kernel_spmd

    nc = bacc.Bacc("TRN2", target_bir_lowering=False, num_devices=1, dynamic_dma_scratch_size=1024)
    chan, spot = np.arange(P), np.arange(P)
    arrays = {
        "x": np.ascontiguousarray(x),
        "weight": np.ascontiguousarray(L0_conv_weight),
        "bias": np.ascontiguousarray(L0_conv_bias_p),
        "ident": np.eye(P, dtype=np.float16),
        "avg_chan": ((chan[:, None] // BLOCK == spot[None, :] // BLOCK) / BLOCK).astype(np.float32),
        "avg_block": ((chan[:, None] // BLOCK == spot[None, :] % GROUPS) / BLOCK).astype(np.float32),
    }
    args = [nc.dram_tensor(n, a.shape, mybir.dt.from_np(a.dtype), kind="ExternalInput").ap() for n, a in arrays.items()]
    out = nc.dram_tensor("out", _OUT, F32, kind="ExternalOutput").ap()
    conv_kernel(nc, *args, out)
    r = run_bass_kernel_spmd(nc, [arrays], core_ids=[0])
    return r.results[0]["out"]
```

```python
from contextlib import ExitStack

import numpy as np

import concourse.bass as bass
from concourse import mybir

ALU = mybir.AluOpType
ACT = mybir.ActivationFunctionType
F32 = mybir.dt.float32
F16 = mybir.dt.float16
U32 = mybir.dt.uint32
U8 = mybir.dt.uint8

P = 128
IMAGES, H, W = 16, 112, 112
PIX = H * W
BLOCK = 4
GROUPS = P // BLOCK
TAPS = 9
EPS = 1e-5

CHUNKS = 7
CROWS = H // CHUNKS
CPIX = CROWS * W
QUARTERS = P // GROUPS
QPIX = CPIX // QUARTERS
PAIRS = CROWS // 2
QUADS = 2
QROWS = CROWS // QUADS
QP = QROWS // 2
TPIX = QP * W
BN = 448
BNS = CPIX // BN
DVE_STATS, ACT_STATS = (0, 4, 6), (1, 2, 3, 5)

XSCALE = 128.0
WSCALE = 4096.0
TINY = 2.0 ** -100
MSCALE = 2.0 ** -13



def conv_kernel(nc, x, weight, bias, ident, inject, avg_chan, avg_block, out):
    x_chan = x.rearrange("b c h w -> b c (h w)")
    out_chan = out.rearrange("b c h w -> b c (h w)")
    x_block = x.rearrange("b (g j) h w -> b g j (h w)", j=BLOCK)
    w_rows = weight.rearrange("o c kh kw -> o (c kh kw)")
    bias_col = bias.rearrange("(p a) -> p a", a=1)

    with ExitStack() as ctx:
        def sb(name, shape, dt):
            return ctx.enter_context(nc.sbuf_tensor(name, shape, dt))

        def sem(name):
            return ctx.enter_context(nc.semaphore(name))

        xs = sb("xs", [P, 2, PIX], F32)
        x16 = sb("x16", [P, 2, H + 2, W], F16)
        v16 = sb("v16", [P, 2, 4, 2, PAIRS, W], F16)
        m16 = sb("m16", [P, 2, TPIX], F16)
        xb = sb("xb", [P, BLOCK, QPIX], F32)
        tmp = sb("tmp", [P, BLOCK, QPIX], F32)
        mask_b = sb("mask_b", [P, BLOCK, QPIX], U8)
        mask_c = sb("mask_c", [P, CPIX], U8)
        z = sb("z", [P, CPIX], F32)
        stage = sb("stage", [P, CROWS, W], F32)
        w_hi = sb("w_hi", [P, TAPS, P], F16)
        w_lo = sb("w_lo", [P, 2, 3, P], F16)
        w_sum = sb("w_sum", [P, 2, 2, 3, P], F16)
        ident_s = sb("ident_s", [P, P], F16)
        inject_s = sb("inject_s", [P, 2, P], F16)
        avg_c = sb("avg_c", [P, P], F32)
        avg_b = sb("avg_b", [P, P], F32)
        bias_s = sb("bias_s", [P, 1], F32)
        w_pow = sb("w_pow", [P, 4], F32)
        NBN = 2 * BNS * len(DVE_STATS)
        NACT = len(ACT_STATS)
        tuples = sb("tuples", [P, NBN + NACT, 3], F32)
        act_sums = sb("act_sums", [P, 2, NACT], F32)
        shift = sb("shift", [P, 1], F32)
        tuple_tmp = sb("tuple_tmp", [P, 2, NACT], F32)
        junk = sb("junk", [P, CPIX], F16)
        cstat = sb("cstat", [P, 2], F32)
        small = sb("small", [P, 6], F32)
        params = sb("params", [P, 2, 3], F32)

        banks = ctx.enter_context(nc.psum_tensor("banks", [P, 2, 4, 512], F32))
        w_trans = banks[:, :, :, :].rearrange("p a b n -> p (a b) n").bitcast(F16)
        mean_c_ps = banks[:, 0, 3, TPIX:TPIX + 1]
        mean_b_ps = banks[:, 0, 3, TPIX + 1:TPIX + 2]
        var_ps = banks[:, 1, 3, TPIX:TPIX + 1]

        at = [0]

        def weight_space(n, dt=F32):
            words = n if dt == F32 else n // 2
            at[0] += words
            view = xs[:, 1, at[0] - words:at[0]]
            return view if dt == F32 else view.bitcast(dt)

        WN = P * TAPS
        wraw, wabs, wmask, wsp, wlo32 = (weight_space(WN) for _ in range(5))
        wmin, wmax = weight_space(WN // 2), weight_space(WN // 2)
        whr, wlr = weight_space(WN, F16), weight_space(WN, F16)
        outer = weight_space(WN // 3)
        wsum = [[weight_space(WN // 3, F16) for _ in range(2)] for _ in range(2)]

        turned = [(whr.rearrange("o (c t) -> o c t", t=TAPS)[:, :, n], w_hi[:, n, :]) for n in range(TAPS)]
        turned += [(wlr.rearrange("o (c t) -> o c t", t=TAPS)[:, :, n], w_lo[:, n // 6, n % 3, :])
                   for n in (0, 1, 2, 6, 7, 8)]
        turned += [(wsum[n][m].rearrange("o (c k) -> o c k", k=3)[:, :, k], w_sum[:, n, m, k, :])
                   for n in range(2) for m in range(2) for k in range(3)]
        WEIGHTS = len(turned)

        consts_in = sem("consts_in")
        x_loaded = [[sem(f"x_loaded{p}{k}") for k in range(CHUNKS)] for p in range(2)]
        stored = [[sem(f"stored{p}{k}") for k in range(CHUNKS)] for p in range(2)]
        xb_loaded = sem("xb_loaded")
        zeroed = sem("zeroed")
        w_step = sem("w_step")
        w_abs_done = sem("w_abs_done")
        w_ready = sem("w_ready")
        w_turned = sem("w_turned")
        w_kept = sem("w_kept")
        w_in = sem("w_in")
        bn_done = sem("bn_done")
        shift_kept = sem("shift_kept")
        act_summed = sem("act_summed")
        mean_part = sem("mean_part")
        square_part = sem("square_part")
        tuples_done = sem("tuples_done")
        counts_set = sem("counts_set")
        chan_stats = sem("chan_stats")
        group_mean = sem("group_mean")
        mean_kept = sem("mean_kept")
        negmean_kept = sem("negmean_kept")
        mean_off = sem("mean_off")
        chan_var = sem("chan_var")
        group_var = sem("group_var")
        var_eps = sem("var_eps")
        root = sem("root")
        inv_root = sem("inv_root")
        root_twice = sem("root_twice")
        inv_twice = sem("inv_twice")
        scale_kept = sem("scale_kept")
        abs_done = sem("abs_done")
        pair_min = sem("pair_min")
        pair_max = sem("pair_max")
        max_of_min = sem("max_of_min")
        min_of_max = sem("min_of_max")
        thr_done = sem("thr_done")
        mask_done = sem("mask_done")
        mask_out_done = sem("mask_out_done")
        mask_moved = sem("mask_moved")
        z_done = sem("z_done")
        hi_done = sem("hi_done")
        lo_done = sem("lo_done")
        v_done = sem("v_done")
        m_done = sem("m_done")
        m_kept = sem("m_kept")
        quad_done = sem("quad_done")
        set_free = sem("set_free")
        stage_free = sem("stage_free")

        mask_dram = nc.dram_tensor("mask_dram", (QUARTERS, P * QPIX), U8).ap()
        mask_out = mask_dram.rearrange("q (g n) -> (q g) n", g=GROUPS)
        mask_in = mask_dram.rearrange("q (p n) -> p q n", n=QPIX)

        block = ctx.enter_context(nc.Block())

        def slots(eng, slot):
            def image(i, p):
                b = 2 * i + p
                for s in range(CHUNKS):
                    slot(i, b, p, s, CHUNKS * b + s)

            with eng.Fori(0, IMAGES // 2 - 1) as i:
                image(i, 0)
                image(i, 1)
            image(IMAGES // 2 - 1, 0)
            image(IMAGES // 2 - 1, 1)

        def exists(c):
            return not isinstance(c, int) or c < IMAGES * CHUNKS

        def ahead(i, p, s, n):
            m = CHUNKS * p + s + n
            return i + m // (2 * CHUNKS), m // CHUNKS % 2, m % CHUNKS

        def pix(k):
            return slice(k * CPIX, (k + 1) * CPIX)

        def rows(part, k):
            return x16[:, part, 1 + k * CROWS:1 + (k + 1) * CROWS, :].rearrange("p h w -> p (h w)")

        @block.sync
        def _(sp):
            def load_block(b, k):
                for q in range(QUARTERS):
                    px = slice(k * CPIX + q * QPIX, k * CPIX + (q + 1) * QPIX)
                    sp.dma_start(xb[GROUPS * q:GROUPS * (q + 1), :, :],
                                 x_block[b, :, :, px]).then_inc(xb_loaded, 16)

            def move_mask(c, following):
                sp.wait_ge(mask_done, c + 1)
                sp.dma_start(mask_out, mask_b[:, :, :].rearrange("p j n -> p (j n)")).then_inc(mask_out_done, 16)
                sp.wait_ge(mask_out_done, 16 * (c + 1))
                sp.dma_start(mask_c[:, :].rearrange("p (q n) -> p q n", q=QUARTERS), mask_in).then_inc(mask_moved, 16)
                if following is not None:
                    load_block(*following)

            sp.dma_start(wraw, w_rows).then_inc(w_in, 16)
            sp.dma_start(bias_s[:, :], bias_col).then_inc(consts_in, 16)
            sp.dma_start(ident_s[:, :], ident).then_inc(consts_in, 16)
            sp.dma_start(inject_s[:, :, :], inject).then_inc(consts_in, 16)
            sp.dma_start(avg_c[:, :], avg_chan).then_inc(consts_in, 16)
            sp.dma_start(avg_b[:, :], avg_block).then_inc(consts_in, 16)
            load_block(0, 0)
            for c in range(4):
                move_mask(c, (0, c + 1))

            def slot(i, b, p, s, t):
                if exists(t + 4):
                    fi, fp, fk = ahead(i, p, s, 5)
                    move_mask(t + 4, (2 * fi + fp, fk) if exists(t + 5) else None)

            slots(sp, slot)

        @block.gpsimd
        def _(pool):
            for k in range(CHUNKS):
                pool.dma_start(xs[:, 0, pix(k)], x_chan[0, :, pix(k)]).then_inc(x_loaded[0][k], 16)
            nc.gpsimd.memset(x16[:, :, 0, :], 0.0).then_inc(zeroed, 1)
            nc.gpsimd.memset(x16[:, :, H + 1, :], 0.0).then_inc(zeroed, 1)
            for n in range(NACT):
                nc.gpsimd.memset(tuples[:, NBN + n, 0:1], float(CPIX)).then_inc(counts_set, 1)
            pool.wait_ge(w_turned, WEIGHTS)
            for k in range(CHUNKS):
                pool.dma_start(xs[:, 1, pix(k)], x_chan[1, :, pix(k)]).then_inc(x_loaded[1][k], 16)

            def slot(i, b, p, s, t):
                pool.wait_ge(stage_free, t + 2)
                pool.dma_start(out_chan[b, :, pix(s)], xs[:, p, pix(s)]).then_inc(stored[p][s], 16)
                if exists(t + 2 * CHUNKS):
                    pool.wait_ge(stored[p][s], 16 * (i + 1))
                    pool.dma_start(xs[:, p, pix(s)], x_chan[b + 2, :, pix(s)]).then_inc(x_loaded[p][s], 16)

            slots(pool, slot)
            for p in range(2):
                for k in range(CHUNKS):
                    pool.wait_ge(stored[p][k], 16 * (IMAGES // 2))

        @block.scalar
        def _(act):
            def absolute(c, i, p, k):
                act.wait_ge(xb_loaded, 64 * (c + 1))
                if k == 0:
                    act.wait_ge(negmean_kept, 2 * i + p + 1)
                nc.scalar.activation(xb[:, :, :], xb[:, :, :], ACT.Abs, bias=params[:, p, 1:2],
                                     scale=1.0).then_inc(abs_done, 1)

            def high(c, i, p, k):
                act.wait_ge(z_done, c + 1)
                if k == 0:
                    act.wait_ge(scale_kept, 2 * i + p + 1)
                nc.scalar.activation(rows(0, k), z[:, :], ACT.Copy, scale=params[:, p, 2:3]).then_inc(hi_done, 1)

            def square_root(n):
                act.wait_ge(var_eps, n + 1)
                nc.scalar.activation(small[:, 3:4], small[:, 2:3], ACT.Sqrt).then_inc(root, 1)

            def keep_m(t, q):
                act.wait_ge(m_done, QUADS * t + q + 1)
                nc.scalar.activation(m16[:, :, :], banks[:, q, 2:4, 0:TPIX], ACT.Copy,
                                     scale=MSCALE).then_inc(m_kept, 1)

            def evacuate(t, q):
                act.wait_ge(quad_done, QUADS * t + q + 1)
                if q == 0:
                    act.wait_ge(stage_free, t + 1)
                dst = stage[:, q * QROWS:(q + 1) * QROWS, :].rearrange("p (r e) w -> p e r w", e=2)
                src = banks[:, q, 0:2, 0:TPIX].rearrange("p e (r w) -> p e r w", w=W)
                nc.scalar.activation(dst, src, ACT.Identity, bias=bias_s[:, 0:1],
                                     scale=w_pow[:, 3:4]).then_inc(set_free, 1)

            def sums(i, p, k, square):
                n = ACT_STATS.index(k)
                if not square:
                    act.wait_ge(x_loaded[p][k], 16 * (i + 1))
                    if n == 0:
                        act.wait_ge(shift_kept, 2 * i + p + 1)
                before = 2 * (NACT * (2 * i + p) + n) + int(square)
                if not isinstance(before, int) or before > 0:
                    act.wait_ge(act_summed, before)
                nc.scalar.activation(junk[:, :], xs[:, p, pix(k)], ACT.Square if square else ACT.Identity,
                                     bias=shift[:, 0:1], scale=1.0,
                                     accum_out=act_sums[:, int(square), n:n + 1]).then_inc(act_summed, 1)

            act.sem_inc(set_free, 2)
            act.wait_ge(w_in, 16)
            nc.scalar.activation(wabs, wraw, ACT.Abs).then_inc(w_abs_done, 1)
            for k in ACT_STATS:
                sums(0, 0, k, False)
                sums(0, 0, k, True)
            square_root(0)
            for c in range(3):
                absolute(c, 0, 0, c)
                high(c, 0, 0, c)
            absolute(3, 0, 0, 3)
            for k in ACT_STATS:
                if k < 12 - CHUNKS:
                    sums(0, 1, k, False)
                    sums(0, 1, k, True)
            absolute(4, 0, 0, 4)
            act.wait_ge(consts_in, 80)

            def slot(i, b, p, s, t):
                stat = ahead(i, p, s, 12)
                summed = exists(t + 12) and stat[2] in ACT_STATS
                if s == 3 and exists(t + CHUNKS):
                    square_root(b + 1)
                keep_m(t, 0)
                evacuate(t, 0)
                if summed:
                    sums(*stat, False)
                keep_m(t, 1)
                if exists(t + 3):
                    high(t + 3, *ahead(i, p, s, 3))
                if summed:
                    sums(*stat, True)
                evacuate(t, 1)
                if exists(t + 5):
                    absolute(t + 5, *ahead(i, p, s, 5))

            slots(act, slot)

        @block.vector
        def _(dve):
            V = nc.vector

            def stats(i, p, k):
                if k not in DVE_STATS:
                    return
                dve.wait_ge(x_loaded[p][k], 16 * (i + 1))
                for m in range(BNS):
                    px = k * CPIX + m * BN
                    at = 2 * (DVE_STATS.index(k) * BNS + m)
                    ins = V.bn_stats(out=tuples[:, at:at + 2, :].rearrange("p a b -> p (a b)"), in_=xs[:, p, px:px + BN])
                ins.then_inc(bn_done, 1)
                if k == 0:
                    dve.wait_ge(bn_done, len(DVE_STATS) * (2 * i + p) + 1)
                    V.tensor_scalar(shift[:, :], tuples[:, 0, 1:2], -1.0, None, ALU.mult).then_inc(shift_kept, 1)

            def finish_tuples(n):
                dve.wait_ge(act_summed, 2 * NACT * (n + 1))
                V.tensor_scalar(tuple_tmp[:, 0, :], act_sums[:, 0, :], 1.0 / CPIX, None, ALU.mult).then_inc(mean_part, 1)
                dve.wait_ge(mean_part, n + 1)
                V.tensor_tensor(tuple_tmp[:, 1, :], act_sums[:, 0, :], tuple_tmp[:, 0, :], ALU.mult).then_inc(square_part, 1)
                V.tensor_scalar(tuples[:, NBN:, 1], tuple_tmp[:, 0, :], shift[:, 0:1], None, ALU.subtract).then_inc(tuples_done, 1)
                dve.wait_ge(square_part, n + 1)
                V.tensor_tensor(tuples[:, NBN:, 2], act_sums[:, 1, :], tuple_tmp[:, 1, :], ALU.subtract).then_inc(tuples_done, 1)

            def tuples_ready(n):
                dve.wait_ge(tuples_done, 2 * (n + 1))
                dve.wait_ge(bn_done, len(DVE_STATS) * (n + 1))

            def channel_stats():
                V.bn_aggr(out=cstat[:, :], in_=tuples[:, :, :].rearrange("p a b -> p (a b)")).then_inc(chan_stats, 1)

            def keep_means(n, p):
                dve.wait_ge(group_mean, n + 1)
                V.tensor_copy(params[:, p, 0:1], mean_c_ps).then_inc(mean_kept, 1)
                V.tensor_scalar(params[:, p, 1:2], mean_b_ps, -1.0, None, ALU.mult).then_inc(negmean_kept, 1)
                dve.wait_ge(mean_kept, n + 1)
                V.tensor_tensor(small[:, 0:1], cstat[:, 0:1], params[:, p, 0:1], ALU.subtract).then_inc(mean_off, 1)
                dve.wait_ge(mean_off, n + 1)
                V.scalar_tensor_tensor(out=small[:, 1:2], in0=small[:, 0:1], scalar=small[:, 0:1],
                                       in1=cstat[:, 1:2], op0=ALU.mult, op1=ALU.add).then_inc(chan_var, 1)

            def keep_var(n):
                dve.wait_ge(group_var, n + 1)
                V.tensor_scalar(small[:, 2:3], var_ps, EPS, None, ALU.add).then_inc(var_eps, 1)

            def keep_scale(n, p):
                dve.wait_ge(root, n + 1)
                V.reciprocal(small[:, 4:5], small[:, 3:4]).then_inc(inv_root, 1)
                dve.wait_ge(inv_root, n + 1)
                V.scalar_tensor_tensor(out=small[:, 5:6], in0=small[:, 2:3], scalar=small[:, 4:5],
                                       in1=small[:, 3:4], op0=ALU.mult, op1=ALU.add).then_inc(root_twice, 1)
                dve.wait_ge(root_twice, n + 1)
                V.reciprocal(small[:, 4:5], small[:, 5:6]).then_inc(inv_twice, 1)
                dve.wait_ge(inv_twice, n + 1)
                V.tensor_scalar(params[:, p, 2:3], small[:, 4:5], 2.0 * XSCALE, None, ALU.mult).then_inc(scale_kept, 1)

            def find_mask(c):
                dve.wait_ge(abs_done, c + 1)
                V.tensor_tensor(tmp[:, 0:2, :], xb[:, 0:2, :], xb[:, 2:4, :], ALU.min).then_inc(pair_min, 1)
                V.tensor_tensor(tmp[:, 2:4, :], xb[:, 0:2, :], xb[:, 2:4, :], ALU.max).then_inc(pair_max, 1)
                dve.wait_ge(pair_min, c + 1)
                V.tensor_tensor(tmp[:, 0, :], tmp[:, 0, :], tmp[:, 1, :], ALU.max).then_inc(max_of_min, 1)
                dve.wait_ge(pair_max, c + 1)
                V.tensor_tensor(tmp[:, 2, :], tmp[:, 2, :], tmp[:, 3, :], ALU.min).then_inc(min_of_max, 1)
                dve.wait_ge(max_of_min, c + 1)
                dve.wait_ge(min_of_max, c + 1)
                V.tensor_tensor(tmp[:, 1, :], tmp[:, 0, :], tmp[:, 2, :], ALU.max).then_inc(thr_done, 1)
                dve.wait_ge(thr_done, c + 1)
                V.tensor_tensor(mask_b[:, :, :], xb[:, :, :], tmp[:, 1:2, :].to_broadcast([P, BLOCK, QPIX]),
                                ALU.is_ge).then_inc(mask_done, 1)

            def sparse(c, i, p, k):
                dve.wait_ge(mask_moved, 16 * (c + 1))
                V.scalar_tensor_tensor(out=z[:, :], in0=xs[:, p, pix(k)], scalar=params[:, p, 0:1],
                                       in1=mask_c[:, :], op0=ALU.subtract, op1=ALU.mult).then_inc(z_done, 1)

            def low(c, i, p, k):
                dve.wait_ge(hi_done, c + 1)
                V.scalar_tensor_tensor(out=rows(1, k), in0=z[:, :], scalar=params[:, p, 2:3], in1=rows(0, k),
                                       op0=ALU.mult, op1=ALU.subtract).then_inc(lo_done, 1)

            def combine(c, i, p, k, lows):
                dve.wait_ge(lo_done, lows)
                ring = (p * CHUNKS + k) % 2
                d0, d1, d2, d3 = (x16[:, :, k * CROWS + n:k * CROWS + n + CROWS - 1:2, :] for n in range(4))
                V.tensor_tensor(v16[:, ring, 0], d0, d2, ALU.subtract)
                V.tensor_tensor(v16[:, ring, 1], d1, d2, ALU.add)
                V.tensor_tensor(v16[:, ring, 2], d2, d1, ALU.subtract)
                V.tensor_tensor(v16[:, ring, 3], d3, d1, ALU.subtract).then_inc(v_done, 1)

            def residual(t, k, p):
                dve.wait_ge(set_free, QUADS * (t + 1) + 2)
                V.tensor_tensor(xs[:, p, pix(k)], xs[:, p, pix(k)], stage[:, :, :].rearrange("p h w -> p (h w)"),
                                ALU.add).then_inc(stage_free, 1)

            dve.sem_inc(stage_free, 1)
            steps = [0]

            def step(ins, wait=True):
                steps[0] += 1
                ins.then_inc(w_step, 1)
                if wait:
                    dve.wait_ge(w_step, steps[0])

            def by_four(v):
                return v.rearrange("o (g j t) -> o g j t", j=BLOCK, t=TAPS)

            def by_two(v):
                return v.rearrange("o (g j t) -> o g j t", j=2, t=TAPS)

            def tap_row(v, n):
                return v.rearrange("o (c r k) -> o c r k", r=3, k=3)[:, :, n, :]

            w_thr, w_min = by_two(wmin)[:, :, 0, :], by_two(wmax)[:, :, 0, :]
            outer3 = outer.rearrange("o (c k) -> o c k", k=3)

            def sparse_weights():
                dve.wait_ge(w_abs_done, 1)
                step(V.tensor_tensor(by_two(wmin), by_four(wabs)[:, :, 0:2, :], by_four(wabs)[:, :, 2:4, :], ALU.min),
                     wait=False)
                step(V.tensor_tensor(by_two(wmax), by_four(wabs)[:, :, 0:2, :], by_four(wabs)[:, :, 2:4, :], ALU.max))
                step(V.tensor_tensor(w_thr, w_thr, by_two(wmin)[:, :, 1, :], ALU.max), wait=False)
                step(V.tensor_tensor(w_min, w_min, by_two(wmax)[:, :, 1, :], ALU.min))
                step(V.tensor_tensor(w_thr, w_thr, w_min, ALU.max))
                for j in range(BLOCK):
                    step(V.tensor_tensor(by_four(wmask)[:, :, j, :], by_four(wabs)[:, :, j, :], w_thr, ALU.is_ge),
                         wait=False)
                step(V.tensor_reduce(w_pow[:, 0:1], wabs, mybir.AxisListType.X, ALU.max))
                step(V.tensor_tensor(wsp, wraw, wmask, ALU.mult), wait=False)
                step(V.tensor_scalar(w_pow[:, 0:1], w_pow[:, 0:1], TINY, None, ALU.max))
                step(V.tensor_scalar(w_pow[:, 1:2].bitcast(U32), w_pow[:, 0:1].bitcast(U32), 0x7F800000, None,
                                     ALU.bitwise_and))
                step(V.reciprocal(w_pow[:, 2:3], w_pow[:, 1:2]), wait=False)
                step(V.tensor_scalar(w_pow[:, 3:4], w_pow[:, 1:2], 1.0 / (XSCALE * WSCALE), None, ALU.mult))

            def split_weights():
                step(V.tensor_scalar(wsp, wsp, w_pow[:, 2:3], WSCALE, ALU.mult, ALU.mult))
                step(V.tensor_copy(whr, wsp))
                step(V.tensor_tensor(wlo32, wsp, whr, ALU.subtract))
                step(V.tensor_copy(wlr, wlo32), wait=False)
                for n, w in enumerate((wsp, wlo32)):
                    step(V.tensor_tensor(outer3, tap_row(w, 0), tap_row(w, 2), ALU.add))
                    for m, op in enumerate((ALU.add, ALU.subtract)):
                        step(V.tensor_tensor(wsum[n][m].rearrange("o (c k) -> o c k", k=3), outer3, tap_row(w, 1), op),
                             wait=m == 1)
                dve.sem_inc(w_ready, 1)

            def turn_weights():
                for n, (src, dst) in enumerate(turned):
                    dve.wait_ge(w_turned, n + 1)
                    V.tensor_copy(dst, w_trans[:, n % 8, 0:P]).then_inc(w_kept, 1)

            stats(0, 0, 0)
            sparse_weights()
            stats(0, 0, 4)
            split_weights()
            stats(0, 0, 6)
            finish_tuples(0)
            dve.wait_ge(counts_set, NACT)
            tuples_ready(0)
            turn_weights()
            channel_stats()
            keep_means(0, 0)
            keep_var(0)
            keep_scale(0, 0)
            dve.wait_ge(zeroed, 2)
            for c in range(3):
                find_mask(c)
                if c == 0:
                    stats(0, 1, 0)
                if c == 1:
                    stats(0, 1, 4)
                sparse(c, 0, 0, c)
                low(c, 0, 0, c)
                if c:
                    combine(c - 1, 0, 0, c - 1, c + 1)
            find_mask(3)

            def slot(i, b, p, s, t):
                if s == 2 and exists(t + CHUNKS):
                    finish_tuples(b + 1)
                    tuples_ready(b + 1)
                if s == 3 and exists(t + CHUNKS):
                    keep_var(b + 1)
                if exists(t + 3):
                    sparse(t + 3, *ahead(i, p, s, 3))
                if s == 2 and exists(t + CHUNKS):
                    channel_stats()
                if exists(t + 4):
                    find_mask(t + 4)
                if s == 2 and exists(t + CHUNKS):
                    keep_means(b + 1, 1 - p)
                if s == 3 and exists(t + CHUNKS):
                    keep_scale(b + 1, 1 - p)
                if exists(t + 12):
                    stats(*ahead(i, p, s, 12))
                if exists(t + 3):
                    low(t + 3, *ahead(i, p, s, 3))
                if exists(t + 2):
                    dve.wait_ge(quad_done, QUADS * (t + 1))
                    combine(t + 2, *ahead(i, p, s, 2), t + 4 if exists(t + 3) else t + 3)
                residual(t, s, p)

            slots(dve, slot)

        @block.tensor
        def _(pe):
            def mean_products(n):
                pe.wait_ge(chan_stats, n + 1)
                nc.tensor.matmul(mean_c_ps, avg_c[:, :], cstat[:, 0:1], start=True, stop=True)
                nc.tensor.matmul(mean_b_ps, avg_b[:, :], cstat[:, 0:1], start=True, stop=True).then_inc(group_mean, 1)

            def var_product(n):
                pe.wait_ge(chan_var, n + 1)
                nc.tensor.matmul(var_ps, avg_c[:, :], small[:, 1:2], start=True, stop=True).then_inc(group_var, 1)

            def quad(t, p, s, q):
                r0 = s * CROWS + q * QROWS
                ring = (p * CHUNKS + s) % 2
                bank = [banks[:, q, n, 0:TPIX].rearrange("p (r w) -> p r w", w=W) for n in range(4)]

                def product(dst, w, src, dx, **flags):
                    u, v = max(0, -dx), min(W, W - dx)
                    return nc.tensor.matmul(dst[:, :, u:v], w, src[:, :, u + dx:v + dx], **flags)

                def correction(dst, kind, lo_w, hi_w, start, stop=False):
                    for dx in (0, -1, 1):
                        for part, w in ((0, lo_w), (1, hi_w)):
                            ins = product(dst, w(dx), v16[:, ring, kind, part, q * QP:(q + 1) * QP, :], dx,
                                          start=start and dx == 0 and part == 0,
                                          stop=stop and dx == 1 and part == 1)
                    return ins

                pe.wait_ge(set_free, QUADS * t + q + 1)
                for m in range(2):
                    ins = correction(bank[2 + m], 1 + m, lambda dx: w_sum[:, 1, m, dx + 1, :],
                                     lambda dx: w_sum[:, 0, m, dx + 1, :], True, True)
                ins.then_inc(m_done, 1)
                for odd in range(2):
                    for n, (dy, dx) in enumerate(sorted(((dy, dx) for dy in (-1, 0, 1) for dx in (-1, 0, 1)),
                                                        key=lambda d: d != (0, 0))):
                        r = 1 + r0 + odd + dy
                        product(bank[odd], w_hi[:, (dy + 1) * 3 + dx + 1, :], x16[:, 0, r:r + QROWS - 1:2, :], dx,
                                start=n == 0, stop=False)
                    correction(bank[odd], 3 * odd, lambda dx: w_lo[:, odd, dx + 1, :],
                               lambda dx: w_hi[:, 6 * odd + dx + 1, :], False)
                pe.wait_ge(m_kept, QUADS * t + q + 1)
                for odd in range(2):
                    for m in range(2):
                        ins = nc.tensor.matmul(banks[:, q, odd, 0:TPIX], inject_s[:, odd & m, :], m16[:, m, :],
                                               start=False, stop=m == 1)
                ins.then_inc(quad_done, 1)

            pe.wait_ge(consts_in, 80)
            pe.wait_ge(w_ready, 1)
            for n, (src, dst) in enumerate(turned):
                if n >= 8:
                    pe.wait_ge(w_kept, n - 7)
                nc.tensor.transpose(w_trans[:, n % 8, 0:P], src, ident_s[:, :]).then_inc(w_turned, 1)
            pe.wait_ge(w_kept, WEIGHTS)
            mean_products(0)
            var_product(0)
            pe.wait_ge(var_eps, 1)

            def slot(i, b, p, s, t):
                pe.wait_ge(v_done, t + 1)
                more = exists(t + CHUNKS)
                if s == 3 and more:
                    pe.wait_ge(negmean_kept, b + 2)
                quad(t, p, s, 0)
                if s == 2 and more:
                    mean_products(b + 1)
                if s == 3 and more:
                    pe.wait_ge(var_eps, b + 2)
                quad(t, p, s, 1)
                if s == 2 and more:
                    var_product(b + 1)

            slots(pe, slot)


_OUT = (IMAGES, P, H, W)


def kernel(x, L0_conv_weight, L0_conv_bias_p):
    import concourse.bacc as bacc
    from concourse.bass_utils import run_bass_kernel_spmd

    nc = bacc.Bacc("TRN2", target_bir_lowering=False, num_devices=1, dynamic_dma_scratch_size=1024)
    chan, spot = np.arange(P), np.arange(P)
    eye = np.eye(P, dtype=np.float16)
    inject = eye * np.float16(0.5 / MSCALE)
    arrays = {
        "x": np.ascontiguousarray(x),
        "weight": np.ascontiguousarray(L0_conv_weight),
        "bias": np.ascontiguousarray(L0_conv_bias_p),
        "ident": eye,
        "inject": np.stack([inject, -inject], axis=1),
        "avg_chan": ((chan[:, None] // BLOCK == spot[None, :] // BLOCK) / BLOCK).astype(np.float32),
        "avg_block": ((chan[:, None] // BLOCK == spot[None, :] % GROUPS) / BLOCK).astype(np.float32),
    }
    args = [nc.dram_tensor(n, a.shape, mybir.dt.from_np(a.dtype), kind="ExternalInput").ap() for n, a in arrays.items()]
    out = nc.dram_tensor("out", _OUT, F32, kind="ExternalOutput").ap()
    conv_kernel(nc, *args, out)
    r = run_bass_kernel_spmd(nc, [arrays], core_ids=[0])
    return r.results[0]["out"]
```

```python
from contextlib import ExitStack

import numpy as np

import concourse.bass as bass
from concourse import mybir

ALU = mybir.AluOpType
ACT = mybir.ActivationFunctionType
F32 = mybir.dt.float32
F16 = mybir.dt.float16
U32 = mybir.dt.uint32
U8 = mybir.dt.uint8

P = 128
IMAGES, H, W = 16, 112, 112
PIX = H * W
BLOCK = 4
GROUPS = P // BLOCK
TAPS = 9
EPS = 1e-5

CHUNKS = 7
CROWS = H // CHUNKS
CPIX = CROWS * W
QUARTERS = P // GROUPS
QPIX = CPIX // QUARTERS
PAIRS = CROWS // 2
QUADS = 2
QROWS = CROWS // QUADS
QP = QROWS // 2
TPIX = QP * W
BN = 448
BNS = CPIX // BN
SETS = 4

XSCALE = 128.0
WSCALE = 4096.0
TINY = 2.0 ** -100
MSCALE = 2.0 ** -13



def conv_kernel(nc, x, weight, bias, ident, inject, avg_chan, avg_block, out):
    x_chan = x.rearrange("b c h w -> b c (h w)")
    out_chan = out.rearrange("b c h w -> b c (h w)")
    x_block = x.rearrange("b (g j) h w -> b g j (h w)", j=BLOCK)
    w_rows = weight.rearrange("o c kh kw -> o (c kh kw)")
    bias_col = bias.rearrange("(p a) -> p a", a=1)

    with ExitStack() as ctx:
        def sb(name, shape, dt):
            return ctx.enter_context(nc.sbuf_tensor(name, shape, dt))

        def sem(name):
            return ctx.enter_context(nc.semaphore(name))

        xs = sb("xs", [P, 2, PIX], F32)
        x16 = sb("x16", [P, 2, H + 2, W], F16)
        v16 = sb("v16", [P, 2, 4, 2, PAIRS, W], F16)
        m16 = sb("m16", [P, 3, TPIX], F16)
        xb = sb("xb", [P, BLOCK, QPIX], F32)
        tmp = sb("tmp", [P, BLOCK, QPIX], F32)
        mask_b = sb("mask_b", [P, BLOCK, QPIX], U8)
        mask_c = sb("mask_c", [P, CPIX], U8)
        z = sb("z", [P, CPIX], F32)
        stage = sb("stage", [P, CROWS, W], F32)
        w_hi = sb("w_hi", [P, TAPS, P], F16)
        w_lo = sb("w_lo", [P, 2, 3, P], F16)
        w_sum = sb("w_sum", [P, 2, 2, 3, P], F16)
        ident_s = sb("ident_s", [P, P], F16)
        inject_s = sb("inject_s", [P, 2, P], F16)
        avg_c = sb("avg_c", [P, P], F32)
        avg_b = sb("avg_b", [P, P], F32)
        bias_s = sb("bias_s", [P, 1], F32)
        w_pow = sb("w_pow", [P, 4], F32)
        shift = sb("shift", [P, 1], F32)
        sums = sb("sums", [P, 2, CHUNKS], F32)
        tuples = sb("tuples", [P, CHUNKS, 3], F32)
        tuple_tmp = sb("tuple_tmp", [P, 2, CHUNKS], F32)
        first_part = sb("first_part", [P, 6], F32)
        parts = sb("parts", [P, 2 * BNS, 3], F32)
        part_stat = sb("part_stat", [P, 4], F32)
        junk = sb("junk", [P, CPIX], F16)
        cstat = sb("cstat", [P, 2], F32)
        small = sb("small", [P, 6], F32)
        params = sb("params", [P, 2, 3], F32)

        banks = ctx.enter_context(nc.psum_tensor("banks", [P, SETS, 2, 512], F32))
        w_trans = banks[:, :, :, :].rearrange("p a b n -> p (a b) n").bitcast(F16)

        def stat_cell(b_set, n):
            return banks[:, b_set, 1, TPIX + n:TPIX + n + 1]

        weight_space = v16[:, :, :, :, :, :].rearrange("p r v n h w -> p (r v n h w)").bitcast(F32)
        WN = P * TAPS

        def weight_view(start, n):
            return weight_space[:, start * WN // 2:start * WN // 2 + n]

        wraw, wabs, wmask, wsp = (weight_view(n, WN) for n in (0, 2, 4, 6))
        wmin, wmax = weight_view(8, WN // 2), weight_view(9, WN // 2)
        whr, wlr = (weight_view(n, WN // 2).bitcast(F16) for n in (10, 11))
        wlo32, outer = weight_view(2, WN), weight_view(8, WN // 3)
        wsum = [[weight_view(4 + n, WN // 2)[:, m * WN // 6:(m + 1) * WN // 6].bitcast(F16) for m in range(2)]
                for n in range(2)]

        by_tap = [v.rearrange("o (c t) -> o t c", t=TAPS) for v in (whr, wlr)]
        by_col = [[wsum[n][m].rearrange("o (c k) -> o k c", k=3) for m in range(2)] for n in range(2)]
        turned = [
            (0, [by_tap[0][:, n, :] for n in range(5)], w_hi[:, 0:5, :], 1.0),
            (1, [by_tap[0][:, n, :] for n in range(5, TAPS)], w_hi[:, 5:TAPS, :], 1.0),
            (2, [by_tap[1][:, n, :] for n in (0, 1, 2, 6, 7, 8)],
             w_lo[:, :, :, :].rearrange("p a k o -> p (a k) o"), 1.0),
            (3, [by_col[0][m][:, k, :] for m in range(2) for k in range(3)],
             w_sum[:, 0].rearrange("p m k o -> p (m k) o"), 0.5),
            (4, [by_col[1][m][:, k, :] for m in range(2) for k in range(3)],
             w_sum[:, 1].rearrange("p m k o -> p (m k) o"), 0.5)]

        first_blocks = [xb[:, :, :], stage[:, :, :].rearrange("p h w -> p (h w)").rearrange("p (j n) -> p j n", j=BLOCK),
                        xs[:, 1, PIX - CPIX:PIX].rearrange("p (j n) -> p j n", j=BLOCK), xb[:, :, :]]

        consts_in = sem("consts_in")
        x_loaded = [[sem(f"x_loaded{p}{k}") for k in range(CHUNKS)] for p in range(2)]
        stored = [[sem(f"stored{p}{k}") for k in range(CHUNKS)] for p in range(2)]
        xb_loaded = sem("xb_loaded")
        early_loaded = [sem("early_loaded1"), sem("early_loaded2")]
        zeroed = sem("zeroed")
        w_step = sem("w_step")
        w_abs_done = sem("w_abs_done")
        w_sparse = sem("w_sparse")
        w_split = sem("w_split")
        w_ready = sem("w_ready")
        w_turned = sem("w_turned")
        w_kept = sem("w_kept")
        w_in = sem("w_in")
        first_done = sem("first_done")
        parts_done = sem("parts_done")
        part_step = sem("part_step")
        shift_kept = sem("shift_kept")
        summed = sem("summed")
        mean_part = sem("mean_part")
        square_part = sem("square_part")
        tuples_done = sem("tuples_done")
        counts_set = sem("counts_set")
        chan_stats = sem("chan_stats")
        group_mean = sem("group_mean")
        mean_kept = sem("mean_kept")
        negmean_kept = sem("negmean_kept")
        mean_off = sem("mean_off")
        chan_var = sem("chan_var")
        group_var = sem("group_var")
        var_eps = sem("var_eps")
        root = sem("root")
        inv_root = sem("inv_root")
        root_twice = sem("root_twice")
        inv_twice = sem("inv_twice")
        scale_kept = sem("scale_kept")
        abs_done = sem("abs_done")
        pair_min = sem("pair_min")
        pair_max = sem("pair_max")
        max_of_min = sem("max_of_min")
        min_of_max = sem("min_of_max")
        thr_done = sem("thr_done")
        mask_done = sem("mask_done")
        mask_out_done = sem("mask_out_done")
        mask_moved = sem("mask_moved")
        z_done = sem("z_done")
        hi_done = sem("hi_done")
        lo_done = sem("lo_done")
        v_done = sem("v_done")
        m1_done = sem("m1_done")
        both_done = sem("both_done")
        m1_kept = sem("m1_kept")
        both_kept = sem("both_kept")
        quad_done = sem("quad_done")
        set_free = sem("set_free")
        stage_free = sem("stage_free")

        mask_dram = nc.dram_tensor("mask_dram", (QUARTERS, P * QPIX), U8).ap()
        mask_out = mask_dram.rearrange("q (g n) -> (q g) n", g=GROUPS)
        mask_in = mask_dram.rearrange("q (p n) -> p q n", n=QPIX)

        block = ctx.enter_context(nc.Block())

        def slots(eng, slot):
            def image(i, p):
                b = 2 * i + p
                for s in range(CHUNKS):
                    slot(i, b, p, s, CHUNKS * b + s)

            with eng.Fori(0, IMAGES // 2 - 1) as i:
                image(i, 0)
                image(i, 1)
            image(IMAGES // 2 - 1, 0)
            image(IMAGES // 2 - 1, 1)

        def exists(c):
            return not isinstance(c, int) or c < IMAGES * CHUNKS

        def bank_set(p, s, q):
            return (QUADS * (p * CHUNKS + s) + q) % SETS

        def sums_before(n, k):
            return 2 * CHUNKS * n - 10 + 2 * k

        def ahead(i, p, s, n):
            m = CHUNKS * p + s + n
            return i + m // (2 * CHUNKS), m // CHUNKS % 2, m % CHUNKS

        def pix(k):
            return slice(k * CPIX, (k + 1) * CPIX)

        def rows(part, k):
            return x16[:, part, 1 + k * CROWS:1 + (k + 1) * CROWS, :].rearrange("p h w -> p (h w)")

        @block.sync
        def _(sp):
            def load_block(b, k, dst, done):
                for q in range(QUARTERS):
                    px = slice(k * CPIX + q * QPIX, k * CPIX + (q + 1) * QPIX)
                    sp.dma_start(dst[GROUPS * q:GROUPS * (q + 1), :, :], x_block[b, :, :, px]).then_inc(done, 16)

            def move_mask(c, following):
                sp.wait_ge(mask_done, c + 1)
                sp.dma_start(mask_out, mask_b[:, :, :].rearrange("p j n -> p (j n)")).then_inc(mask_out_done, 16)
                if following is not None:
                    load_block(*following, xb[:, :, :], xb_loaded)
                sp.wait_ge(mask_out_done, 16 * (c + 1))
                if isinstance(c, int) and c == 1:
                    sp.wait_ge(z_done, 1)
                sp.dma_start(mask_c[:, :].rearrange("p (q n) -> p q n", q=QUARTERS), mask_in).then_inc(mask_moved, 16)

            sp.dma_start(wraw, w_rows).then_inc(w_in, 16)
            sp.dma_start(bias_s[:, :], bias_col).then_inc(consts_in, 16)
            sp.dma_start(ident_s[:, :], ident).then_inc(consts_in, 16)
            sp.dma_start(inject_s[:, :, :], inject).then_inc(consts_in, 16)
            sp.dma_start(avg_c[:, :], avg_chan).then_inc(consts_in, 16)
            sp.dma_start(avg_b[:, :], avg_block).then_inc(consts_in, 16)
            sp.wait_ge(x_loaded[0][CHUNKS - 3], 16)
            load_block(0, 0, first_blocks[0], xb_loaded)
            load_block(0, 1, first_blocks[1], early_loaded[0])
            load_block(0, 2, first_blocks[2], early_loaded[1])
            move_mask(0, None)
            load_block(0, 3, xb[:, :, :], xb_loaded)
            sp.wait_ge(mask_moved, 16)
            move_mask(1, None)
            move_mask(2, None)
            move_mask(3, (0, 4))

            def slot(i, b, p, s, t):
                if exists(t + 4):
                    fi, fp, fk = ahead(i, p, s, 5)
                    move_mask(t + 4, (2 * fi + fp, fk) if exists(t + 5) else None)

            slots(sp, slot)

        @block.gpsimd
        def _(pool):
            def tap_row(v, n):
                return v.rearrange("o (c r k) -> o c r k", r=3, k=3)[:, :, n, :]

            steps = [0]

            def step(ins, wait=True):
                steps[0] += 1
                ins.then_inc(w_split, 1)
                if wait:
                    pool.wait_ge(w_split, steps[0])

            G = nc.gpsimd

            def split_weights():
                pool.wait_ge(w_sparse, 1)
                step(G.tensor_scalar(wsp, wsp, w_pow[:, 2:3], WSCALE, ALU.mult, ALU.mult))
                step(G.tensor_copy(whr, wsp))
                step(G.tensor_tensor(wlo32, wsp, whr, ALU.subtract))
                step(G.tensor_copy(wlr, wlo32))

            def sum_weights():
                outer3 = outer.rearrange("o (c k) -> o c k", k=3)
                for n, w in enumerate((wsp, wlo32)):
                    step(G.tensor_tensor(outer3, tap_row(w, 0), tap_row(w, 2), ALU.add))
                    for m, op in enumerate((ALU.add, ALU.subtract)):
                        step(G.tensor_tensor(wsum[n][m].rearrange("o (c k) -> o c k", k=3), outer3, tap_row(w, 1), op),
                             wait=m == 1)
                pool.sem_inc(w_ready, 1)

            def second_image(*chunks):
                for k in chunks:
                    pool.dma_start(xs[:, 1, pix(k)], x_chan[1, :, pix(k)]).then_inc(x_loaded[1][k], 16)

            for k in range(CHUNKS):
                pool.dma_start(xs[:, 0, pix(k)], x_chan[0, :, pix(k)]).then_inc(x_loaded[0][k], 16)
            nc.gpsimd.memset(x16[:, :, 0, :], 0.0).then_inc(zeroed, 1)
            nc.gpsimd.memset(x16[:, :, H + 1, :], 0.0).then_inc(zeroed, 1)
            for k in range(CHUNKS):
                nc.gpsimd.memset(tuples[:, k, 0:1], float(CPIX)).then_inc(counts_set, 1)
            split_weights()
            pool.wait_ge(early_loaded[1], 64)
            second_image(0, 1)
            sum_weights()
            pool.wait_ge(mask_moved, 16)
            second_image(2)
            pool.wait_ge(mask_moved, 32)
            second_image(3, 4)
            pool.wait_ge(mask_moved, 48)
            second_image(5, 6)

            def slot(i, b, p, s, t):
                pool.wait_ge(stage_free, t + 2)
                pool.dma_start(out_chan[b, :, pix(s)], xs[:, p, pix(s)]).then_inc(stored[p][s], 16)
                if exists(t + 2 * CHUNKS):
                    pool.wait_ge(stored[p][s], 16 * (i + 1))
                    pool.dma_start(xs[:, p, pix(s)], x_chan[b + 2, :, pix(s)]).then_inc(x_loaded[p][s], 16)

            slots(pool, slot)
            for p in range(2):
                for k in range(CHUNKS):
                    pool.wait_ge(stored[p][k], 16 * (IMAGES // 2))

        @block.scalar
        def _(act):
            def absolute(c, i, p, k, blk=xb[:, :, :]):
                if isinstance(c, int) and c in (1, 2):
                    act.wait_ge(early_loaded[c - 1], 64)
                elif isinstance(c, int) and c == 0:
                    act.wait_ge(xb_loaded, 64)
                else:
                    act.wait_ge(xb_loaded, 64 * (c - 1))
                if k == 0:
                    act.wait_ge(negmean_kept, 2 * i + p + 1)
                nc.scalar.activation(blk, blk, ACT.Abs, bias=params[:, p, 1:2], scale=1.0).then_inc(abs_done, 1)

            def high(c, i, p, k):
                act.wait_ge(z_done, c + 1)
                if k == 0:
                    act.wait_ge(scale_kept, 2 * i + p + 1)
                nc.scalar.activation(rows(0, k), z[:, :], ACT.Copy, scale=params[:, p, 2:3]).then_inc(hi_done, 1)

            def square_root(n):
                act.wait_ge(var_eps, n + 1)
                nc.scalar.activation(small[:, 3:4], small[:, 2:3], ACT.Sqrt).then_inc(root, 1)

            def keep_m1(t, p, s, q):
                act.wait_ge(m1_done, QUADS * t + q + 1)
                nc.scalar.activation(m16[:, q, :], banks[:, bank_set(p, s, q), 0, 0:TPIX], ACT.Copy,
                                     scale=MSCALE).then_inc(m1_kept, 1)

            def keep_both(t, p, s, q):
                act.wait_ge(both_done, QUADS * t + q + 1)
                nc.scalar.activation(m16[:, 2, :], banks[:, bank_set(p, s, q), 0, 0:TPIX], ACT.Copy,
                                     scale=MSCALE).then_inc(both_kept, 1)

            def evacuate(t, p, s, q):
                act.wait_ge(quad_done, QUADS * t + q + 1)
                if q == 0:
                    act.wait_ge(stage_free, t + 1)
                dst = stage[:, q * QROWS:(q + 1) * QROWS, :].rearrange("p (r e) w -> p e r w", e=2)
                src = banks[:, bank_set(p, s, q), :, 0:TPIX].rearrange("p e (r w) -> p e r w", w=W)
                nc.scalar.activation(dst, src, ACT.Identity, bias=bias_s[:, 0:1],
                                     scale=w_pow[:, 3:4]).then_inc(set_free, 1)

            def add_up(i, p, k, square, before):
                if not square:
                    act.wait_ge(x_loaded[p][k], 16 * (i + 1))
                    act.wait_ge(shift_kept, 2 * i + p + 1)
                if not isinstance(before, int) or before > 0:
                    act.wait_ge(summed, before)
                nc.scalar.activation(junk[:, :], xs[:, p, pix(k)], ACT.Square if square else ACT.Identity,
                                     bias=shift[:, 0:1], scale=1.0,
                                     accum_out=sums[:, int(square), k:k + 1]).then_inc(summed, 1)

            act.sem_inc(set_free, SETS)
            act.wait_ge(w_in, 16)
            nc.scalar.activation(wabs, wraw, ACT.Abs).then_inc(w_abs_done, 1)
            for n, k in enumerate((1, 2, 3, 5)):
                add_up(0, 0, k, False, 2 * n)
                add_up(0, 0, k, True, 2 * n + 1)
            absolute(0, 0, 0, 0, first_blocks[0])
            square_root(0)
            absolute(1, 0, 0, 1, first_blocks[1])
            for n, (bank, srcs, dst, factor) in enumerate(turned):
                act.wait_ge(w_turned, n + 1)
                src = w_trans[:, bank, 0:len(srcs) * P].rearrange("p (n o) -> p n o", o=P)
                nc.scalar.activation(dst, src, ACT.Copy, scale=factor).then_inc(w_kept, 1)
            absolute(2, 0, 0, 2, first_blocks[2])
            high(0, 0, 0, 0)
            add_up(0, 1, 1, False, 8)
            add_up(0, 1, 1, True, 9)
            absolute(3, 0, 0, 3, first_blocks[3])
            high(1, 0, 0, 1)
            for k in (2, 3):
                add_up(0, 1, k, False, 6 + 2 * k)
                add_up(0, 1, k, True, 7 + 2 * k)
            high(2, 0, 0, 2)
            act.wait_ge(consts_in, 80)
            keep_m1(0, 0, 0, 0)

            def slot(i, b, p, s, t):
                fi, fp, fk = ahead(i, p, s, 12)
                before = sums_before(2 * fi + fp, fk)
                keep_both(t, p, s, 0)
                keep_m1(t, p, s, 1)
                if s == 3 and exists(t + CHUNKS):
                    square_root(b + 1)
                if exists(t + 4):
                    absolute(t + 4, *ahead(i, p, s, 4))
                if exists(t + 12):
                    add_up(fi, fp, fk, False, before)
                evacuate(t, p, s, 0)
                keep_both(t, p, s, 1)
                if exists(t + 1):
                    ni, nq, nk = ahead(i, p, s, 1)
                    keep_m1(t + 1, nq, nk, 0)
                if exists(t + 3):
                    high(t + 3, *ahead(i, p, s, 3))
                if exists(t + 12):
                    add_up(fi, fp, fk, True, before + 1)
                evacuate(t, p, s, 1)

            slots(act, slot)

        @block.vector
        def _(dve):
            V = nc.vector

            def keep_shift(i, p):
                dve.wait_ge(x_loaded[p][0], 16 * (i + 1))
                V.bn_stats(out=first_part[:, :], in_=xs[:, p, 0:BN]).then_inc(first_done, 1)
                dve.wait_ge(first_done, 2 * i + p + 1)
                V.tensor_scalar(shift[:, :], first_part[:, 1:2], -1.0, None, ALU.mult).then_inc(shift_kept, 1)

            part_steps = [0]

            def part_stats(p, k):
                def step(ins):
                    part_steps[0] += 1
                    ins.then_inc(part_step, 1)
                    dve.wait_ge(part_step, part_steps[0])

                dve.wait_ge(x_loaded[p][k], 16)
                for m in range(BNS):
                    px = k * CPIX + m * BN
                    ins = V.bn_stats(out=parts[:, 2 * m:2 * m + 2, :].rearrange("p a b -> p (a b)"),
                                     in_=xs[:, p, px:px + BN])
                step(ins)
                step(V.bn_aggr(out=part_stat[:, 0:2], in_=parts[:, :, :].rearrange("p a b -> p (a b)")))
                step(V.tensor_tensor(part_stat[:, 2:3], part_stat[:, 0:1], shift[:, 0:1], ALU.add))
                V.tensor_scalar(sums[:, 0, k:k + 1], part_stat[:, 2:3], float(CPIX), None, ALU.mult).then_inc(parts_done, 1)
                step(V.scalar_tensor_tensor(out=part_stat[:, 3:4], in0=part_stat[:, 2:3], scalar=part_stat[:, 2:3],
                                            in1=part_stat[:, 1:2], op0=ALU.mult, op1=ALU.add))
                V.tensor_scalar(sums[:, 1, k:k + 1], part_stat[:, 3:4], float(CPIX), None, ALU.mult).then_inc(parts_done, 1)

            def finish_tuples(n, before):
                dve.wait_ge(summed, before)
                V.tensor_scalar(tuple_tmp[:, 0, :], sums[:, 0, :], 1.0 / CPIX, None, ALU.mult).then_inc(mean_part, 1)
                dve.wait_ge(mean_part, n + 1)
                V.tensor_tensor(tuple_tmp[:, 1, :], sums[:, 0, :], tuple_tmp[:, 0, :], ALU.mult).then_inc(square_part, 1)
                V.tensor_scalar(tuples[:, :, 1], tuple_tmp[:, 0, :], shift[:, 0:1], None, ALU.subtract).then_inc(tuples_done, 1)
                dve.wait_ge(square_part, n + 1)
                V.tensor_tensor(tuples[:, :, 2], sums[:, 1, :], tuple_tmp[:, 1, :], ALU.subtract).then_inc(tuples_done, 1)
                dve.wait_ge(tuples_done, 2 * (n + 1))

            def channel_stats():
                V.bn_aggr(out=cstat[:, :], in_=tuples[:, :, :].rearrange("p a b -> p (a b)")).then_inc(chan_stats, 1)

            def keep_means(n, p, b_set):
                dve.wait_ge(group_mean, n + 1)
                V.tensor_copy(params[:, p, 0:1], stat_cell(b_set, 0)).then_inc(mean_kept, 1)
                V.tensor_scalar(params[:, p, 1:2], stat_cell(b_set, 1), -1.0, None, ALU.mult).then_inc(negmean_kept, 1)
                dve.wait_ge(mean_kept, n + 1)
                V.tensor_tensor(small[:, 0:1], cstat[:, 0:1], params[:, p, 0:1], ALU.subtract).then_inc(mean_off, 1)
                dve.wait_ge(mean_off, n + 1)
                V.scalar_tensor_tensor(out=small[:, 1:2], in0=small[:, 0:1], scalar=small[:, 0:1],
                                       in1=cstat[:, 1:2], op0=ALU.mult, op1=ALU.add).then_inc(chan_var, 1)

            def keep_var(n, b_set):
                dve.wait_ge(group_var, n + 1)
                V.tensor_scalar(small[:, 2:3], stat_cell(b_set, 2), EPS, None, ALU.add).then_inc(var_eps, 1)

            def keep_scale(n, p):
                dve.wait_ge(root, n + 1)
                V.reciprocal(small[:, 4:5], small[:, 3:4]).then_inc(inv_root, 1)
                dve.wait_ge(inv_root, n + 1)
                V.scalar_tensor_tensor(out=small[:, 5:6], in0=small[:, 2:3], scalar=small[:, 4:5],
                                       in1=small[:, 3:4], op0=ALU.mult, op1=ALU.add).then_inc(root_twice, 1)
                dve.wait_ge(root_twice, n + 1)
                V.reciprocal(small[:, 4:5], small[:, 5:6]).then_inc(inv_twice, 1)
                dve.wait_ge(inv_twice, n + 1)
                V.tensor_scalar(params[:, p, 2:3], small[:, 4:5], 2.0 * XSCALE, None, ALU.mult).then_inc(scale_kept, 1)

            def compare(c, blk=xb[:, :, :]):
                dve.wait_ge(abs_done, c + 1)
                if isinstance(c, int) and 1 <= c < 4:
                    dve.wait_ge(mask_done, c)
                V.tensor_tensor(tmp[:, 0:2, :], blk[:, 0:2, :], blk[:, 2:4, :], ALU.min).then_inc(pair_min, 1)
                V.tensor_tensor(tmp[:, 2:4, :], blk[:, 0:2, :], blk[:, 2:4, :], ALU.max).then_inc(pair_max, 1)
                dve.wait_ge(pair_min, c + 1)
                V.tensor_tensor(tmp[:, 0, :], tmp[:, 0, :], tmp[:, 1, :], ALU.max).then_inc(max_of_min, 1)
                dve.wait_ge(pair_max, c + 1)
                V.tensor_tensor(tmp[:, 2, :], tmp[:, 2, :], tmp[:, 3, :], ALU.min).then_inc(min_of_max, 1)

            def threshold(c, blk=xb[:, :, :]):
                dve.wait_ge(max_of_min, c + 1)
                dve.wait_ge(min_of_max, c + 1)
                V.tensor_tensor(tmp[:, 1, :], tmp[:, 0, :], tmp[:, 2, :], ALU.max).then_inc(thr_done, 1)
                dve.wait_ge(thr_done, c + 1)
                if isinstance(c, int) and c == 1:
                    dve.wait_ge(mask_out_done, 16)
                V.tensor_tensor(mask_b[:, :, :], blk, tmp[:, 1:2, :].to_broadcast([P, BLOCK, QPIX]),
                                ALU.is_ge).then_inc(mask_done, 1)

            def sparse(c, i, p, k):
                dve.wait_ge(mask_moved, 16 * (c + 1))
                if isinstance(c, int) and c == 1:
                    dve.wait_ge(lo_done, c)
                V.scalar_tensor_tensor(out=z[:, :], in0=xs[:, p, pix(k)], scalar=params[:, p, 0:1],
                                       in1=mask_c[:, :], op0=ALU.subtract, op1=ALU.mult).then_inc(z_done, 1)

            def low(c, i, p, k):
                dve.wait_ge(hi_done, c + 1)
                V.scalar_tensor_tensor(out=rows(1, k), in0=z[:, :], scalar=params[:, p, 2:3], in1=rows(0, k),
                                       op0=ALU.mult, op1=ALU.subtract).then_inc(lo_done, 1)

            def combine(c, i, p, k, lows):
                dve.wait_ge(lo_done, lows)
                ring = (p * CHUNKS + k) % 2
                d0, d1, d2, d3 = (x16[:, :, k * CROWS + n:k * CROWS + n + CROWS - 1:2, :] for n in range(4))
                V.tensor_tensor(v16[:, ring, 0], d0, d2, ALU.subtract)
                V.tensor_tensor(v16[:, ring, 1], d1, d2, ALU.add)
                V.tensor_tensor(v16[:, ring, 2], d2, d1, ALU.subtract)
                V.tensor_tensor(v16[:, ring, 3], d3, d1, ALU.subtract).then_inc(v_done, 1)

            def residual(t, k, p):
                dve.wait_ge(set_free, QUADS * (t + 1) + SETS)
                V.tensor_tensor(xs[:, p, pix(k)], xs[:, p, pix(k)], stage[:, :, :].rearrange("p h w -> p (h w)"),
                                ALU.add).then_inc(stage_free, 1)

            dve.sem_inc(stage_free, 1)
            steps = [0]

            def step(ins, wait=True):
                steps[0] += 1
                ins.then_inc(w_step, 1)
                if wait:
                    dve.wait_ge(w_step, steps[0])

            def by_four(v):
                return v.rearrange("o (g j t) -> o g j t", j=BLOCK, t=TAPS)

            def by_two(v):
                return v.rearrange("o (g j t) -> o g j t", j=2, t=TAPS)

            w_thr, w_min = by_two(wmin)[:, :, 0, :], by_two(wmax)[:, :, 0, :]

            def sparse_weights():
                dve.wait_ge(w_abs_done, 1)
                step(V.tensor_tensor(by_two(wmin), by_four(wabs)[:, :, 0:2, :], by_four(wabs)[:, :, 2:4, :], ALU.min),
                     wait=False)
                step(V.tensor_tensor(by_two(wmax), by_four(wabs)[:, :, 0:2, :], by_four(wabs)[:, :, 2:4, :], ALU.max))
                step(V.tensor_tensor(w_thr, w_thr, by_two(wmin)[:, :, 1, :], ALU.max), wait=False)
                step(V.tensor_tensor(w_min, w_min, by_two(wmax)[:, :, 1, :], ALU.min))
                step(V.tensor_tensor(w_thr, w_thr, w_min, ALU.max))
                for j in range(BLOCK):
                    step(V.tensor_tensor(by_four(wmask)[:, :, j, :], by_four(wabs)[:, :, j, :], w_thr, ALU.is_ge),
                         wait=False)
                step(V.tensor_reduce(w_pow[:, 0:1], wabs, mybir.AxisListType.X, ALU.max))
                step(V.tensor_tensor(wsp, wraw, wmask, ALU.mult), wait=False)
                step(V.tensor_scalar(w_pow[:, 0:1], w_pow[:, 0:1], TINY, None, ALU.max))
                step(V.tensor_scalar(w_pow[:, 1:2].bitcast(U32), w_pow[:, 0:1].bitcast(U32), 0x7F800000, None,
                                     ALU.bitwise_and))
                step(V.reciprocal(w_pow[:, 2:3], w_pow[:, 1:2]), wait=False)
                step(V.tensor_scalar(w_pow[:, 3:4], w_pow[:, 1:2], 1.0 / (XSCALE * WSCALE), None, ALU.mult))
                dve.sem_inc(w_sparse, 1)

            keep_shift(0, 0)
            part_stats(0, 0)
            sparse_weights()
            part_stats(0, 4)
            part_stats(0, 6)
            dve.wait_ge(counts_set, CHUNKS)
            dve.wait_ge(parts_done, 6)
            finish_tuples(0, 8)
            channel_stats()
            keep_means(0, 0, SETS - 1)
            keep_var(0, SETS - 1)
            compare(0, first_blocks[0])
            keep_scale(0, 0)
            threshold(0, first_blocks[0])
            compare(1, first_blocks[1])
            threshold(1, first_blocks[1])
            sparse(0, 0, 0, 0)
            keep_shift(0, 1)
            compare(2, first_blocks[2])
            dve.wait_ge(zeroed, 2)
            low(0, 0, 0, 0)
            sparse(1, 0, 0, 1)
            threshold(2, first_blocks[2])
            low(1, 0, 0, 1)
            dve.wait_ge(w_turned, len(turned))
            combine(0, 0, 0, 0, 2)
            sparse(2, 0, 0, 2)
            compare(3, first_blocks[3])
            threshold(3, first_blocks[3])
            low(2, 0, 0, 2)
            combine(1, 0, 0, 1, 3)
            part_stats(1, 0)
            part_stats(1, 4)

            def slot(i, b, p, s, t):
                more = exists(t + CHUNKS)
                if exists(t + 4):
                    compare(t + 4)
                if s == 2 and more:
                    keep_means(b + 1, 1 - p, bank_set(p, s, -1))
                if s == 3 and more:
                    keep_scale(b + 1, 1 - p)
                if exists(t + 3):
                    sparse(t + 3, *ahead(i, p, s, 3))
                if exists(t + 4):
                    threshold(t + 4)
                if exists(t + 3):
                    low(t + 3, *ahead(i, p, s, 3))
                if s == 1 and more:
                    finish_tuples(b + 1, sums_before(b + 2, 0))
                if s == 2 and more:
                    keep_var(b + 1, bank_set(p, s, 0))
                if exists(t + 2):
                    dve.wait_ge(quad_done, QUADS * (t + 1))
                    combine(t + 2, *ahead(i, p, s, 2), t + 4 if exists(t + 3) else t + 3)
                if s == 1 and more:
                    channel_stats()
                if s == 1 and exists(t + 2 * CHUNKS):
                    keep_shift(i + 1, p)
                residual(t, s, p)

            slots(dve, slot)

        @block.tensor
        def _(pe):
            def mean_products(n, b_set):
                pe.wait_ge(chan_stats, n + 1)
                nc.tensor.matmul(stat_cell(b_set, 0), avg_c[:, :], cstat[:, 0:1], start=True, stop=True)
                nc.tensor.matmul(stat_cell(b_set, 1), avg_b[:, :], cstat[:, 0:1], start=True,
                                 stop=True).then_inc(group_mean, 1)

            def var_product(n, b_set):
                pe.wait_ge(chan_var, n + 1)
                nc.tensor.matmul(stat_cell(b_set, 2), avg_c[:, :], small[:, 1:2], start=True,
                                 stop=True).then_inc(group_var, 1)


            def product(dst, w, src, dx, start, stop):
                u, v = max(0, -dx), min(W, W - dx)
                return nc.tensor.matmul(dst[:, :, u:v], w, src[:, :, u + dx:v + dx], start=start, stop=stop,
                                        skip_group_check=True)

            def bank(p, s, q, odd):
                return banks[:, bank_set(p, s, q), odd, 0:TPIX].rearrange("p (r w) -> p r w", w=W)

            def main(p, s, q, odd, start):
                zeros = -1 if (s, q, odd) == (0, 0, 0) else 1 if (s, q, odd) == (CHUNKS - 1, QUADS - 1, 1) else None
                taps = [(dy, dx) for dy in (-1, 0, 1) for dx in (-1, 0, 1)]
                taps.sort(key=lambda d: (d != (0, 0), d[1] == 0, d[0] != zeros))
                for n, (dy, dx) in enumerate(taps):
                    u, v = int(dy == zeros == -1), QP - int(dy == zeros == 1)
                    r = 1 + s * CROWS + q * QROWS + odd + dy
                    ins = product(bank(p, s, q, odd)[:, u:v, :], w_hi[:, (dy + 1) * 3 + dx + 1, :],
                                  x16[:, 0, r + 2 * u:r + 2 * v - 1:2, :], dx, start=start and n == 0,
                                  stop=n == TAPS - 1)
                return ins

            def correction(p, s, q, odd, kind, lo_w, hi_w, start=False):
                ring = (p * CHUNKS + s) % 2
                w = (lo_w, hi_w)
                for n, (part, dx) in enumerate(((0, 0), (0, -1), (0, 1), (1, -1), (1, 1), (1, 0))):
                    ins = product(bank(p, s, q, odd), w[part](dx), v16[:, ring, kind, part, q * QP:(q + 1) * QP, :], dx,
                                  start=start and n == 0, stop=n == 5)
                return ins

            def half_sum(m, part):
                return lambda dx: w_sum[:, part, m, dx + 1, :]

            def outer_row(odd):
                return lambda dx: w_lo[:, odd, dx + 1, :], lambda dx: w_hi[:, 6 * odd + dx + 1, :]

            def first_step(t, p, s, q):
                pe.wait_ge(set_free, QUADS * t + q + 1)
                correction(p, s, q, 0, 1, half_sum(0, 1), half_sum(0, 0), start=True).then_inc(m1_done, 1)
                main(p, s, q, 1, True)

            def second_step(t, p, s, q):
                pe.wait_ge(m1_kept, QUADS * t + q + 1)
                correction(p, s, q, 0, 2, half_sum(1, 1), half_sum(1, 0)).then_inc(both_done, 1)
                correction(p, s, q, 1, 3, *outer_row(1))

            def last_step(t, p, s, q):
                pe.wait_ge(both_kept, QUADS * t + q + 1)
                correction(p, s, q, 0, 0, *outer_row(0))
                main(p, s, q, 0, False)
                odd = banks[:, bank_set(p, s, q), 1, 0:TPIX]
                nc.tensor.matmul(odd, inject_s[:, 0, :], m16[:, q, :], start=False, stop=True,
                                 skip_group_check=True)
                nc.tensor.matmul(odd, inject_s[:, 1, :], m16[:, 2, :], start=False, stop=True,
                                 skip_group_check=True).then_inc(quad_done, 1)

            pe.wait_ge(consts_in, 80)
            mean_products(0, SETS - 1)
            var_product(0, SETS - 1)
            pe.wait_ge(w_ready, 1)
            for w_bank, srcs, dst, factor in turned:
                for n, src in enumerate(srcs):
                    ins = nc.tensor.transpose(w_trans[:, w_bank, n * P:(n + 1) * P], src, ident_s[:, :])
                ins.then_inc(w_turned, 1)
            pe.wait_ge(w_kept, len(turned))
            pe.wait_ge(var_eps, 1)
            pe.wait_ge(v_done, 1)
            first_step(0, 0, 0, 0)

            def slot(i, b, p, s, t):
                more = exists(t + CHUNKS)
                second_step(t, p, s, 0)
                if s == 3 and more:
                    pe.wait_ge(negmean_kept, b + 2)
                first_step(t, p, s, 1)
                last_step(t, p, s, 0)
                if s == 2 and more:
                    pe.wait_ge(set_free, QUADS * t + SETS)
                    mean_products(b + 1, bank_set(p, s, -1))
                second_step(t, p, s, 1)
                if s == 3 and more:
                    pe.wait_ge(var_eps, b + 2)
                if exists(t + 1):
                    pe.wait_ge(v_done, t + 2)
                    ni, nq, nk = ahead(i, p, s, 1)
                    first_step(t + 1, nq, nk, 0)
                last_step(t, p, s, 1)
                if s == 2 and more:
                    pe.wait_ge(set_free, QUADS * t + SETS + 1)
                    var_product(b + 1, bank_set(p, s, 0))

            slots(pe, slot)


_OUT = (IMAGES, P, H, W)


def kernel(x, L0_conv_weight, L0_conv_bias_p):
    import concourse.bacc as bacc
    from concourse.bass_utils import run_bass_kernel_spmd

    nc = bacc.Bacc("TRN2", target_bir_lowering=False, num_devices=1, dynamic_dma_scratch_size=1024)
    chan, spot = np.arange(P), np.arange(P)
    eye = np.eye(P, dtype=np.float16)
    inject = eye * np.float16(1.0 / MSCALE)
    arrays = {
        "x": np.ascontiguousarray(x),
        "weight": np.ascontiguousarray(L0_conv_weight),
        "bias": np.ascontiguousarray(L0_conv_bias_p),
        "ident": eye,
        "inject": np.stack([2 * inject, -inject], axis=1),
        "avg_chan": ((chan[:, None] // BLOCK == spot[None, :] // BLOCK) / BLOCK).astype(np.float32),
        "avg_block": ((chan[:, None] // BLOCK == spot[None, :] % GROUPS) / BLOCK).astype(np.float32),
    }
    args = [nc.dram_tensor(n, a.shape, mybir.dt.from_np(a.dtype), kind="ExternalInput").ap() for n, a in arrays.items()]
    out = nc.dram_tensor("out", _OUT, F32, kind="ExternalOutput").ap()
    conv_kernel(nc, *args, out)
    r = run_bass_kernel_spmd(nc, [arrays], core_ids=[0])
    return r.results[0]["out"]
```
